# Optimizing a Trainium2 kernel written in Bass

```python
import numpy as np
import jax
import jax.numpy as jnp

def _softmax(x, axis=-1):
    return jax.nn.softmax(x, axis=axis)

def _gelu(x):
    return jax.nn.gelu(x, approximate=True)

def _silu(x):
    return jax.nn.silu(x)

def _sigmoid(x):
    return jax.nn.sigmoid(x)

def _layernorm(x, axis=-1, eps=1e-05):
    m = jnp.mean(x, axis=axis, keepdims=True)
    v = jnp.var(x, axis=axis, keepdims=True)
    return (x - m) / jnp.sqrt(v + eps)

def _scatter_add(tgt, idx, src, axis=0):
    return tgt.at[idx].add(src)

def _segment_sum(src, seg, n):
    return jax.ops.segment_sum(src, seg, n)
kernel_name = 'mk_xattn_ffn_d1_seqx_r8_256f14'

def setup_inputs(seed: int=0):
    np.random.seed(seed)
    _w = jnp.asarray

    def _rec_inputs():
        import jax
        import jax.numpy as jnp
        _rk = jax.random.key(seed)
        x = -0.000125 + 0.9999 * jax.random.normal(jax.random.fold_in(_rk, 1), (8, 128, 256), jnp.float32)
        _lenS = 128 - jax.random.randint(jax.random.fold_in(_rk, 7), (8,), 0, max(1, 128 // 4) + 1, jnp.int32)
        _lenS2 = 128 - jax.random.randint(jax.random.fold_in(_rk, 8), (8,), 0, max(1, 128 // 4) + 1, jnp.int32)
        _ctx_2048P = jax.random.normal(jax.random.fold_in(_rk, 11), (8, 16, 256), jnp.float32)
        _ctx_2048c = jax.random.dirichlet(jax.random.fold_in(_rk, 511), 0.3 * jnp.ones((16,), jnp.float32), (8, 128))
        _ctx_2048t = jnp.einsum('bsk,bkd->bsd', _ctx_2048c, _ctx_2048P)
        _ctx_2048t = _ctx_2048t * jax.lax.rsqrt(jnp.mean(jnp.square(_ctx_2048t)) + 1e-12) * 0.953939
        ctx_2048 = -0.000514642 + 1.00011 * (_ctx_2048t + 0.3 * jax.random.normal(jax.random.fold_in(_rk, 611), (8, 128, 256), jnp.float32))
        _validS = jnp.arange(128)[None, :] < _lenS[:, None]
        _validS2 = jnp.arange(128)[None, :] < _lenS2[:, None]
        _causal = jnp.tril(jnp.ones((128, 128), dtype=bool))
        mask_BxS2_bk0 = jnp.logical_not(jnp.broadcast_to(_validS2[:, :], (8, 128)))
        return (x, ctx_2048, mask_BxS2_bk0)
    x, ctx_2048, mask_BxS2_bk0 = _rec_inputs()

    def _L0_xattn_setup():
        import jax, jax.numpy as jnp
        import numpy as np
        key = jax.random.key(seed)
        k1, k2, k3 = jax.random.split(key, 3)
        B, S, D, M = (8, 256, 256, 128)
        hidden_states = jax.random.normal(k1, (B, S, D), dtype=jnp.float32)
        memory_tokens = jax.random.normal(k2, (B, M, D), dtype=jnp.float32)
        memory_mask = jax.random.randint(k3, (B, M), 0, 2).astype(jnp.bool_)
        return {'hidden_states': hidden_states, 'memory_tokens': memory_tokens, 'memory_mask': memory_mask}
    _L0_xattn_all = _L0_xattn_setup()
    _L0_xattn_in = {k: v for k, v in _L0_xattn_all.items() if k in ()}
    del _L0_xattn_all

    def _L0_ffn_setup():
        import jax, jax.numpy as jnp
        import numpy as np
        B, S, D, F, E, SH, K = (2, 256, 256, 128, 16, 2, 2)

        def _experts_all(x, g, gb, w1, b1, w2, b2):
            y = jax.nn.gelu(jnp.einsum('bsd,edf->bsef', x, g) + gb, approximate=False)
            y = y * (jnp.einsum('bsd,edf->bsef', x, w1) + b1)
            return jnp.einsum('bsef,efd->bsed', y, w2) + b2
        key = jax.random.key(seed)
        ks = jax.random.split(key, 8)
        std = 0.02
        mk = lambda k, sh: jax.random.normal(k, sh, jnp.float32) * std
        return {'x': jax.random.normal(ks[0], (B, S, D), jnp.float32), 'wa': mk(ks[1], (D, E)), 'rg': mk(ks[2], (E, D, F)), 'rgb': jnp.zeros((E, F), jnp.float32), 'rw1': mk(ks[3], (E, D, F)), 'rb1': jnp.zeros((E, F), jnp.float32), 'rw2': mk(ks[4], (E, F, D)), 'rb2': jnp.zeros((E, D), jnp.float32), 'sg': mk(ks[5], (SH, D, F)), 'sgb': jnp.zeros((SH, F), jnp.float32), 'sw1': mk(ks[6], (SH, D, F)), 'sb1': jnp.zeros((SH, F), jnp.float32), 'sw2': mk(ks[7], (SH, F, D)), 'sb2': jnp.zeros((SH, D), jnp.float32)}
    _L0_ffn_all = _L0_ffn_setup()
    _L0_ffn_in = {k: v for k, v in _L0_ffn_all.items() if k in ('wa', 'rg', 'rgb', 'rw1', 'rb1', 'rw2', 'rb2', 'sg', 'sgb', 'sw1', 'sb1', 'sw2', 'sb2')}
    del _L0_ffn_all
    return {'x': x, 'ctx_2048': ctx_2048, 'mask_BxS2_bk0': mask_BxS2_bk0, 'L0_ffn_wa': _L0_ffn_in['wa'], 'L0_ffn_rg': _L0_ffn_in['rg'], 'L0_ffn_rgb': _L0_ffn_in['rgb'], 'L0_ffn_rw1': _L0_ffn_in['rw1'], 'L0_ffn_rb1': _L0_ffn_in['rb1'], 'L0_ffn_rw2': _L0_ffn_in['rw2'], 'L0_ffn_rb2': _L0_ffn_in['rb2'], 'L0_ffn_sg': _L0_ffn_in['sg'], 'L0_ffn_sgb': _L0_ffn_in['sgb'], 'L0_ffn_sw1': _L0_ffn_in['sw1'], 'L0_ffn_sb1': _L0_ffn_in['sb1'], 'L0_ffn_sw2': _L0_ffn_in['sw2'], 'L0_ffn_sb2': _L0_ffn_in['sb2']}

def reference(x, ctx_2048, mask_BxS2_bk0, L0_ffn_wa, L0_ffn_rg, L0_ffn_rgb, L0_ffn_rw1, L0_ffn_rb1, L0_ffn_rw2, L0_ffn_rb2, L0_ffn_sg, L0_ffn_sgb, L0_ffn_sw1, L0_ffn_sb1, L0_ffn_sw2, L0_ffn_sb2):
    import jax
    import jax.numpy as jnp

    def _L0_xattn_ref(hidden_states, memory_tokens, memory_mask):
        import jax, jax.numpy as jnp
        import numpy as np
        B, S, D = hidden_states.shape
        scale = 1.0 / jnp.sqrt(jnp.asarray(D, hidden_states.dtype))
        scores = jnp.einsum('bsd,bmd->bsm', hidden_states, memory_tokens) * scale
        neg_inf = jnp.asarray(-1e+30, scores.dtype)
        scores = jnp.where(memory_mask[:, None, :], scores, neg_inf)
        attn = jax.nn.softmax(scores, axis=-1)
        readout = jnp.einsum('bsm,bmd->bsd', attn, memory_tokens)
        valid_b = jnp.any(memory_mask, axis=-1)
        out = jnp.where(valid_b[:, None, None], readout, jnp.zeros_like(readout))
        return out

    def _L0_ffn_ref(x, wa, rg, rgb, rw1, rb1, rw2, rb2, sg, sgb, sw1, sb1, sw2, sb2):
        import jax, jax.numpy as jnp
        import numpy as np
        B, S, D, F, E, SH, K = (2, 256, 256, 128, 16, 2, 2)

        def _experts_all(x, g, gb, w1, b1, w2, b2):
            y = jax.nn.gelu(jnp.einsum('bsd,edf->bsef', x, g) + gb, approximate=False)
            y = y * (jnp.einsum('bsd,edf->bsef', x, w1) + b1)
            return jnp.einsum('bsef,efd->bsed', y, w2) + b2
        aff = jax.nn.sigmoid(jnp.einsum('bsd,de->bse', x, wa))
        topk_p, topk_i = jax.lax.top_k(aff, K)
        topk_p = topk_p / jnp.sum(topk_p, axis=-1, keepdims=True)
        combine = jnp.sum(jax.nn.one_hot(topk_i, E, dtype=x.dtype) * topk_p[..., None], axis=2)
        routed = jnp.einsum('bsed,bse->bsd', _experts_all(x, rg, rgb, rw1, rb1, rw2, rb2), combine)
        shared = jnp.sum(_experts_all(x, sg, sgb, sw1, sb1, sw2, sb2), axis=2)
        return x + shared + routed
    x = x + _L0_xattn_ref(_layernorm(x, axis=-1), ctx_2048, mask_BxS2_bk0)
    x = x + _L0_ffn_ref(_layernorm(x, axis=-1), L0_ffn_wa, L0_ffn_rg, L0_ffn_rgb, L0_ffn_rw1, L0_ffn_rb1, L0_ffn_rw2, L0_ffn_rb2, L0_ffn_sg, L0_ffn_sgb, L0_ffn_sw1, L0_ffn_sb1, L0_ffn_sw2, L0_ffn_sb2)
    return x

_drawn_inputs = setup_inputs


def setup_inputs(seed=0):
    import zlib

    import numpy as np

    out = dict(_drawn_inputs(seed))
    spreads = {'L0_ffn_rgb': (0.0, 0.8),
     'L0_ffn_rb1': (0.0, 0.8),
     'L0_ffn_rb2': (0.0, 0.8),
     'L0_ffn_sgb': (0.0, 0.8),
     'L0_ffn_sb1': (0.0, 0.8),
     'L0_ffn_sb2': (0.0, 0.56)}
    factors = {'L0_ffn_rg': 8.0,
     'L0_ffn_rw1': 8.0,
     'L0_ffn_rw2': 8.0,
     'L0_ffn_sg': 6.829,
     'L0_ffn_sw1': 6.594,
     'L0_ffn_sw2': 6.29}
    for name, (base, spread) in spreads.items():
        noise = np.random.default_rng([zlib.crc32(name.encode()), seed]).standard_normal(out[name].shape)
        drawn = base * np.exp(spread * noise) if base else spread * noise
        out[name] = jnp.asarray(drawn.astype(out[name].dtype))
    for name, factor in factors.items():
        out[name] = (out[name] * factor).astype(out[name].dtype)
    return out
```

```python
from contextlib import ExitStack

import concourse.bass as bass
from concourse import mybir

P = 128
F32 = mybir.dt.float32
U8 = mybir.dt.uint8
ALU = mybir.AluOpType
ACT = mybir.ActivationFunctionType
AX = mybir.AxisListType
EPS = 1e-5
NEG = -1e30


def xattn_moe(nc, x, ctx_mem, mask, wa, rg, rgb, rw1, rb1, rw2, rb2, sg, sgb, sw1, sb1, sw2, sb2, out):
    T, S, D = x.shape
    E, _, F = rg.shape
    SH = sg.shape[0]
    EA = E + SH
    KC = D // P
    HALF = T * P // 2
    SCALE = float(D) ** -0.5
    FIRST = 2
    ROUTE_BEST = 12

    def col_of(e):
        return E + e if isinstance(e, int) else e - SH

    assert S == P and F == P and D == 2 * P and SH == 2 and E % 2 == 0

    stack = ExitStack()
    with stack:
        def sb(name, shape, dt=F32):
            return stack.enter_context(nc.sbuf_tensor(name, shape, dt))

        def sem(name):
            return stack.enter_context(nc.semaphore(name))

        bank = [stack.enter_context(nc.psum_tensor(f"bank{i}", [P, 512], F32)) for i in range(8)]

        ident = sb("ident", [P, P])
        power = sb("power", [P, T])
        ones_row = sb("ones_row", [1, P])
        expert_no = sb("expert_no", [P, T, E])
        xs = sb("xs", [P, T, D])
        mem = sb("mem", [P, T, D])
        mask_row = sb("mask_row", [1, T * P], U8)
        wa_sb = sb("wa_sb", [P, KC, E])
        bias_rows = sb("bias_rows", [2 * EA, F])
        b2_rows = sb("b2_rows", [EA, D])
        shut_row = sb("shut_row", [1, T * P])
        any_row = sb("any_row", [1, T])
        any_open = sb("any_open", [P, T])
        stats = sb("stats", [P, T, 6])
        mean_var = sb("mean_var", [P, T, 2])
        var_eps = sb("var_eps", [P, T])
        rstd = sb("rstd", [P, T])
        xn = sb("xn", [P, T, D])
        xm_t = sb("xm_t", [P, T, 4, P])
        row_max = sb("row_max", [P, T])
        neg_max = sb("neg_max", [P, T])
        probs = sb("probs", [P, T, P])
        prob_sum = sb("prob_sum", [P, T])
        prob_inv = sb("prob_inv", [P, T])
        prob_scale = sb("prob_scale", [P, T])
        probs_t = sb("probs_t", [P, T, P])
        acc = sb("acc", [P, T, D])
        stats2 = sb("stats2", [P, T, 6])
        mean_var2 = sb("mean_var2", [P, T, 2])
        var_eps2 = sb("var_eps2", [P, T])
        rstd2 = sb("rstd2", [P, T])
        hn = sb("hn", [P, T, D])
        hn_t = sb("hn_t", [P, KC, T * P])
        logits = sb("logits", [P, T, E])
        hit = sb("hit", [P, T, E])
        place = sb("place", [P, T, E])
        best = sb("best", [P, 2, T])
        best_no = sb("best_no", [P, 2, T])
        chosen = sb("chosen", [P, 2, T, E])
        rest = sb("rest", [P, T, E])
        exp_neg = sb("exp_neg", [P, 2, T])
        one_plus = sb("one_plus", [P, 2, T])
        gate_sum = sb("gate_sum", [P, T])
        gate_inv = sb("gate_inv", [P, T])
        share = sb("share", [P, 2, T])
        part = sb("part", [P, 2, T, E])
        combine = sb("combine", [P, T, EA])
        combine_t = sb("combine_t", [EA, T * P])
        bias_t = sb("bias_t", [P, 2 * EA])
        bias_now = sb("bias_now", [P, 2])
        wg = sb("wg", [P, 2, KC, F])
        wu = sb("wu", [P, 2, KC, F])
        wd = sb("wd", [P, 2, D])
        gated = sb("gated", [P, 2, HALF])
        y_t = sb("y_t", [P, 2, HALF])

        ident_made = sem("ident_made")
        consts = sem("consts")
        power_made = sem("power_made")
        eps_made = sem("eps_made")
        eps2_made = sem("eps2_made")
        x_in = [sem("x_in0"), sem("x_in1")]
        mem_in = [sem("mem_in0"), sem("mem_in1")]
        mask_in = sem("mask_in")
        small_in = sem("small_in")
        w_in = [sem("w_in0"), sem("w_in1")]
        out_done = sem("out_done")
        shut_made = sem("shut_made")
        any_summed = sem("any_summed")
        any_made = sem("any_made")
        stat_made = sem("stat_made")
        aggr_made = sem("aggr_made")
        rstd_made = sem("rstd_made")
        xn_made = sem("xn_made")
        xm_turned = sem("xm_turned")
        xm_copied = sem("xm_copied")
        scores_made = sem("scores_made")
        max_made = sem("max_made")
        neg_made = sem("neg_made")
        probs_made = sem("probs_made")
        probs_turned = sem("probs_turned")
        probs_copied = sem("probs_copied")
        inv_made = sem("inv_made")
        scale_made = sem("scale_made")
        read_made = sem("read_made")
        h_made = sem("h_made")
        stat2_made = sem("stat2_made")
        aggr2_made = sem("aggr2_made")
        rstd2_made = sem("rstd2_made")
        hn_made = sem("hn_made")
        hn_turned = sem("hn_turned")
        hn_copied = sem("hn_copied")
        logits_made = sem("logits_made")
        route = sem("route")
        gate_exp = sem("gate_exp")
        combine_made = sem("combine_made")
        combine_turned = sem("combine_turned")
        combine_copied = sem("combine_copied")
        bias_turned = sem("bias_turned")
        bias_copied = sem("bias_copied")
        hn_added = sem("hn_added")
        b2_made = sem("b2_made")
        b2_added = sem("b2_added")
        bias_picked = sem("bias_picked")
        gate_made = sem("gate_made")
        up_made = sem("up_made")
        gelu_made = sem("gelu_made")
        y_made = sem("y_made")
        down_made = sem("down_made")
        down_added = sem("down_added")

        block = stack.enter_context(nc.Block())

        @block.sync
        def _(sp):
            for g, (a, b) in enumerate(((0, FIRST), (FIRST, T))):
                sp.dma_start(xs[:, a:b, :], x[a:b].rearrange("t p d -> p t d")).then_inc(x_in[g], 16)
                sp.dma_start(mem[:, a:b, :], ctx_mem[a:b].rearrange("t p d -> p t d")).then_inc(mem_in[g], 16)
                if g == 0:
                    sp.dma_start(mask_row[:, :], mask.rearrange("(o t) m -> o (t m)", o=1)).then_inc(mask_in, 16)
            sp.dma_start(wa_sb[:, :, :], wa.rearrange("(c p) e -> p c e", p=P)).then_inc(small_in, 16)
            for row, src in ((0, rgb), (E, sgb), (EA, rb1), (EA + E, sb1)):
                sp.dma_start(bias_rows[row:row + src.shape[0], :], src).then_inc(small_in, 16)
            sp.dma_start(b2_rows[0:E, :], rb2).then_inc(small_in, 16)
            sp.dma_start(b2_rows[E:EA, :], sb2).then_inc(small_in, 16)

            def load_expert(j, g, w1, w2):
                sp.dma_start(wg[:, j, :, :], g.rearrange("o (c p) f -> p (o c) f", p=P)).then_inc(w_in[j], 16)
                sp.dma_start(wu[:, j, :, :], w1.rearrange("o (c p) f -> p (o c) f", p=P)).then_inc(w_in[j], 16)
                sp.dma_start(wd[:, j, :], w2.rearrange("o f d -> f (o d)")).then_inc(w_in[j], 16)

            for j in range(SH):
                load_expert(j, sg[j:j + 1], sw1[j:j + 1], sw2[j:j + 1])
            with sp.Fori(0, E // 2) as n:
                for j in range(2):
                    sp.wait_ge(down_made, 8 * n + 4 * (j + 1))
                    e = bass.ds(2 * n + j, 1)
                    load_expert(j, rg[e], rw1[e], rw2[e])
            sp.wait_ge(down_added, 8 * EA)
            sp.dma_start(out.rearrange("t p d -> p t d"), acc[:, :, :]).then_inc(out_done, 16)
            sp.wait_ge(out_done, 16)

        @block.gpsimd
        def _(pool):
            pool.memset(ident[:, :], 0.0).then_inc(ident_made, 1)
            pool.wait_ge(ident_made, 1)
            pool.affine_select(out=ident[:, :], in_=ident[:, :], compare_op=ALU.not_equal, fill=1.0, base=0,
                               pattern=[[-1, P]], channel_multiplier=1).then_inc(consts, 1)
            pool.memset(ones_row[:, :], 1.0).then_inc(consts, 1)
            pool.iota(expert_no[:, :, :], pattern=[[0, T], [1, E]], base=0, channel_multiplier=0,
                      allow_small_or_imprecise_dtypes=True).then_inc(consts, 1)
            pool.memset(combine[:, :, E:EA], 1.0).then_inc(consts, 1)
            pool.memset(power[:, :], -0.5).then_inc(power_made, 1)
            pool.wait_ge(power_made, 1)

            def inverse_deviation(mv, ve, rs, mv_sem, ve_sem, rs_sem, a, b):
                pool.wait_ge(mv_sem, b)
                pool.tensor_scalar(ve[:, a:b], mv[:, a:b, 1], EPS, None, ALU.add).then_inc(ve_sem, 1)
                pool.wait_ge(ve_sem, 1 if a == 0 else 2)
                pool.tensor_tensor(rs[:, a:b], ve[:, a:b], power[:, a:b], ALU.pow).then_inc(rs_sem, 1)

            for a, b in ((0, FIRST), (FIRST, T)):
                inverse_deviation(mean_var, var_eps, rstd, aggr_made, eps_made, rstd_made, a, b)
            inverse_deviation(mean_var2, var_eps2, rstd2, aggr2_made, eps2_made, rstd2_made, 0, T)
            for t in range(T):
                pool.wait_ge(hn_made, t + 1)
                pool.tensor_tensor(acc[:, t, :], acc[:, t, :], hn[:, t, :], ALU.add).then_inc(hn_added, 1)

        @block.tensor
        def _(pe):
            pe.wait_ge(consts, 4)
            pe.wait_ge(shut_made, 2)
            pe.matmul(bank[7][:, 0:T], ones_row[:, :], any_row[:, :], start=True, stop=True).then_inc(any_summed, 1)
            for t in range(T):
                if t == 0:
                    pe.wait_ge(mem_in[0], 16)
                if t == FIRST:
                    pe.wait_ge(mem_in[1], 16)
                if t >= 2:
                    pe.wait_ge(xm_copied, t - 1)
                for c in range(KC):
                    pe.transpose(bank[t % 2][:, (KC + c) * P:(KC + c + 1) * P], mem[:, t, c * P:(c + 1) * P],
                                 ident[:, :])
                pe.wait_ge(xn_made, t + 1)
                for c in range(KC):
                    mm = pe.transpose(bank[t % 2][:, c * P:(c + 1) * P], xn[:, t, c * P:(c + 1) * P], ident[:, :])
                mm.then_inc(xm_turned, 1)
            for t in range(T):
                pe.wait_ge(xm_copied, t + 1)
                if t >= 2:
                    pe.wait_ge(probs_made, t - 1)
                for c in range(KC):
                    pe.matmul(bank[2 + t % 2][:, 0:P], xm_t[:, t, c, :], xm_t[:, t, KC + c, :],
                              start=(c == 0), stop=False)
                pe.matmul(bank[2 + t % 2][:, 0:P], ones_row[:, :], shut_row[:, t * P:(t + 1) * P],
                          start=False, stop=True).then_inc(scores_made, 1)
            for t in range(T):
                pe.wait_ge(probs_made, t + 1)
                if t >= 2:
                    pe.wait_ge(probs_copied, t - 1)
                pe.transpose(bank[4 + t % 2][:, 0:P], probs[:, t, :], ident[:, :]).then_inc(probs_turned, 1)
            pe.wait_ge(any_made, 1)
            for t in range(T):
                pe.wait_ge(probs_copied, t + 1)
                if t >= 2:
                    pe.wait_ge(h_made, t - 1)
                pe.matmul(bank[6 + t % 2][:, 0:D], probs_t[:, t, :], mem[:, t, :],
                          start=True, stop=True).then_inc(read_made, 1)
            pe.wait_ge(small_in, 7 * 16)
            pe.transpose(bank[4][:, 0:2 * EA], bias_rows[:, :], ident[0:2 * EA, 0:2 * EA]).then_inc(bias_turned, 1)
            for t in range(T):
                pe.wait_ge(hn_made, t + 1)
                if t >= 2:
                    pe.wait_ge(hn_copied, t - 1)
                for c in range(KC):
                    mm = pe.transpose(bank[t % 2][:, c * P:(c + 1) * P], hn[:, t, c * P:(c + 1) * P], ident[:, :])
                mm.then_inc(hn_turned, 1)
            for t in range(T):
                pe.wait_ge(hn_copied, t + 1)
                for c in range(KC):
                    mm = pe.matmul(bank[2][:, t * E:(t + 1) * E], hn_t[:, c, t * P:(t + 1) * P], wa_sb[:, c, :],
                                   start=(c == 0), stop=(c == KC - 1))
            mm.then_inc(logits_made, 1)
            pe.wait_ge(combine_made, 2)
            pe.wait_ge(bias_copied, 1)
            for t in range(T):
                mm = pe.transpose(bank[4 + t // 4][0:EA, (t % 4) * P:(t % 4 + 1) * P], combine[:, t, :], ident[:, :])
            mm.then_inc(combine_turned, 1)
            pe.wait_ge(combine_copied, 2)
            for t in range(T):
                if t >= 4:
                    pe.wait_ge(b2_added, t - 3)
                pe.matmul(bank[4 + t % 4][:, 0:D], combine_t[:, t * P:(t + 1) * P], b2_rows[:, :],
                          start=True, stop=True).then_inc(b2_made, 1)

            def expert(n, j, first):
                e = 2 * n + j
                pe.wait_ge(w_in[j], 48 * (n + 1))
                for h in range(2):
                    if not first:
                        pe.wait_ge(gelu_made, 2 * (e - 1) + h + 1)
                    for c in range(KC):
                        mm = pe.matmul(bank[h][:, :], wg[:, j, c, :], hn_t[:, c, h * HALF:(h + 1) * HALF],
                                       start=(c == 0), stop=(c == KC - 1))
                    mm.then_inc(gate_made, 1)
                    if not first:
                        pe.wait_ge(y_made, 2 * (e - 1) + h + 1)
                    for c in range(KC):
                        mm = pe.matmul(bank[2 + h][:, :], wu[:, j, c, :], hn_t[:, c, h * HALF:(h + 1) * HALF],
                                       start=(c == 0), stop=(c == KC - 1))
                    mm.then_inc(up_made, 1)
                for t in range(T):
                    q, r = t // (T // 2), t % (T // 2)
                    if r == 0:
                        pe.wait_ge(y_made, 2 * e + q + 1)
                    if t % 2 == 0:
                        if first:
                            pe.wait_ge(b2_added, T)
                        else:
                            pe.wait_ge(down_added, 8 * (e - 1) + t + 2)
                    mm = pe.matmul(bank[4 + t // 2][:, (t % 2) * D:(t % 2 + 1) * D],
                                   y_t[:, q, r * P:(r + 1) * P], wd[:, j, :], start=True, stop=True)
                    if t % 2:
                        mm.then_inc(down_made, 1)

            for j in range(SH):
                expert(0, j, j == 0)
            with pe.Fori(1, EA // 2) as n:
                for j in range(2):
                    expert(n, j, False)

        def each_tile(step, first=0, last=T):
            for t in range(first, last):
                step(t, t % 2)

        @block.scalar
        def _(act):
            def copy_inputs(t, j):
                act.wait_ge(xm_turned, t + 1)
                act.copy(xm_t[:, t, :, :], bank[j][:, :]).then_inc(xm_copied, 1)
            each_tile(copy_inputs)

            def exp_scores(t, j):
                act.wait_ge(neg_made, t + 1)
                act.activation(probs[:, t, :], bank[2 + j][:, 0:P], ACT.Exp,
                               bias=neg_max[:, t:t + 1], scale=SCALE,
                               accum_out=prob_sum[:, t:t + 1]).then_inc(probs_made, 1)
            each_tile(exp_scores)

            def copy_probs(t, j):
                act.wait_ge(probs_turned, t + 1)
                act.copy(probs_t[:, t, :], bank[4 + j][:, 0:P]).then_inc(probs_copied, 1)
            each_tile(copy_probs)

            act.wait_ge(bias_turned, 1)
            act.copy(bias_t[:, :], bank[4][:, 0:2 * EA]).then_inc(bias_copied, 1)

            def copy_hn(t, j):
                act.wait_ge(hn_turned, t + 1)
                act.copy(hn_t[:, :, t * P:(t + 1) * P],
                         bank[j][:, 0:D].rearrange("p (c s) -> p c s", c=KC)).then_inc(hn_copied, 1)
            each_tile(copy_hn)

            act.wait_ge(route, ROUTE_BEST)
            act.activation(exp_neg[:, :, :], best[:, :, :], ACT.Exp, scale=-1.0).then_inc(gate_exp, 1)
            act.wait_ge(combine_turned, 1)
            for q in range(2):
                act.copy(combine_t[:, q * HALF:(q + 1) * HALF], bank[4 + q][0:EA, :]).then_inc(combine_copied, 1)

            def expert(n, j, first):
                e = 2 * n + j
                act.wait_ge(gelu_made, 2 * e)
                act.copy(bias_now[:, j:j + 1], bias_t[:, bass.ds(col_of(e), 1)]).then_inc(bias_picked, 1)
                for h in range(2):
                    act.wait_ge(bias_picked, e + 1)
                    act.wait_ge(gate_made, 2 * e + h + 1)
                    if not first:
                        act.wait_ge(y_made, 2 * (e - 1) + h + 1)
                    act.activation(gated[:, h, :], bank[h][:, :], ACT.Gelu,
                                   bias=bias_now[:, j:j + 1]).then_inc(gelu_made, 1)

            for j in range(SH):
                expert(0, j, j == 0)
            with act.Fori(1, EA // 2) as n:
                for j in range(2):
                    expert(n, j, False)

        @block.vector
        def _(dve):
            dve.wait_ge(mask_in, 16)
            dve.tensor_scalar(shut_row[:, :], mask_row[:, :], -NEG / SCALE, NEG / SCALE,
                              ALU.mult, ALU.add).then_inc(shut_made, 1)
            dve.tensor_reduce(any_row[:, :], mask_row[:, :].rearrange("o (t m) -> o t m", t=T), AX.X,
                              ALU.max).then_inc(shut_made, 1)

            def layernorm(src, st, mv, rs, dst, st_sem, mv_sem, rs_sem, dst_sem, a, b, before=None):
                def moments(t, j):
                    if before is not None:
                        before(t, j)
                    dve.bn_stats(st[:, t, :], src[:, t, :]).then_inc(st_sem, 1)
                    dve.wait_ge(st_sem, t + 1)
                    dve.bn_aggr(mv[:, t, :], st[:, t, :]).then_inc(mv_sem, 1)
                each_tile(moments, a, b)
                dve.wait_ge(rs_sem, 1 if a == 0 else 2)

                def normalise(t, j):
                    dve.tensor_scalar(dst[:, t, :], src[:, t, :],
                                      mv[:, t, 0:1], rs[:, t:t + 1],
                                      ALU.subtract, ALU.mult).then_inc(dst_sem, 1)
                each_tile(normalise, a, b)

            for g, (a, b) in enumerate(((0, FIRST), (FIRST, T))):
                dve.wait_ge(x_in[g], 16)
                layernorm(xs, stats, mean_var, rstd, xn, stat_made, aggr_made, rstd_made, xn_made, a, b)
            dve.wait_ge(any_summed, 1)
            dve.tensor_copy(any_open[:, :], bank[7][:, 0:T]).then_inc(any_made, 1)

            def maxima(t, j):
                dve.wait_ge(scores_made, t + 1)
                dve.tensor_reduce(row_max[:, t:t + 1], bank[2 + j][:, 0:P], AX.X, ALU.max).then_inc(max_made, 1)
                dve.wait_ge(max_made, t + 1)
                dve.tensor_scalar(neg_max[:, t:t + 1], row_max[:, t:t + 1], -SCALE, None,
                                  ALU.mult).then_inc(neg_made, 1)
            each_tile(maxima)

            dve.wait_ge(probs_made, T)
            dve.reciprocal(prob_inv[:, :], prob_sum[:, :]).then_inc(inv_made, 1)
            dve.wait_ge(inv_made, 1)
            dve.wait_ge(any_made, 1)
            dve.tensor_tensor(prob_scale[:, :], prob_inv[:, :], any_open[:, :], ALU.mult).then_inc(scale_made, 1)
            dve.wait_ge(scale_made, 1)

            def add_readout(t, j):
                dve.wait_ge(read_made, t + 1)
                dve.scalar_tensor_tensor(out=acc[:, t, :], in0=bank[6 + j][:, 0:D],
                                         scalar=prob_scale[:, t:t + 1], in1=xs[:, t, :],
                                         op0=ALU.mult, op1=ALU.add).then_inc(h_made, 1)
                dve.wait_ge(h_made, t + 1)
            layernorm(acc, stats2, mean_var2, rstd2, hn, stat2_made, aggr2_made, rstd2_made, hn_made, 0, T,
                      before=add_readout)

            step = [0]

            def routed(ins):
                step[0] += 1
                ins.then_inc(route, 1)

            def over_experts(v):
                return v.rearrange("p (t o) -> p t o", o=1).broadcast_to([P, T, E])

            dve.wait_ge(consts, 4)
            dve.wait_ge(logits_made, 1)
            routed(dve.tensor_copy(logits[:, :, :], bank[2][:, 0:T * E]))
            dve.wait_ge(route, 1)
            for k in range(2):
                src = logits if k == 0 else rest
                routed(dve.tensor_reduce(best[:, k, :], src[:, :, :], AX.X, ALU.max))
                dve.wait_ge(route, step[0])
                routed(dve.tensor_tensor(hit[:, :, :], src[:, :, :], over_experts(best[:, k, :]), ALU.is_lt))
                dve.wait_ge(route, step[0])
                routed(dve.scalar_tensor_tensor(out=place[:, :, :], in0=hit[:, :, :], scalar=float(E),
                                                in1=expert_no[:, :, :], op0=ALU.mult, op1=ALU.add))
                dve.wait_ge(route, step[0])
                routed(dve.tensor_reduce(best_no[:, k, :], place[:, :, :], AX.X, ALU.min))
                dve.wait_ge(route, step[0])
                routed(dve.tensor_tensor(chosen[:, k, :, :], expert_no[:, :, :], over_experts(best_no[:, k, :]),
                                         ALU.is_equal))
                dve.wait_ge(route, step[0])
                if k == 0:
                    routed(dve.scalar_tensor_tensor(out=rest[:, :, :], in0=chosen[:, 0, :, :], scalar=-3e38,
                                                    in1=logits[:, :, :], op0=ALU.mult, op1=ALU.add))
                    dve.wait_ge(route, step[0])
            assert step[0] == ROUTE_BEST
            dve.wait_ge(gate_exp, 1)
            routed(dve.tensor_scalar(one_plus[:, :, :], exp_neg[:, :, :], 1.0, None, ALU.add))
            dve.wait_ge(route, step[0])
            routed(dve.reciprocal(exp_neg[:, :, :], one_plus[:, :, :]))
            dve.wait_ge(route, step[0])
            routed(dve.tensor_tensor(gate_sum[:, :], exp_neg[:, 0, :], exp_neg[:, 1, :], ALU.add))
            dve.wait_ge(route, step[0])
            routed(dve.reciprocal(gate_inv[:, :], gate_sum[:, :]))
            dve.wait_ge(route, step[0])
            for k in range(2):
                routed(dve.tensor_tensor(share[:, k, :], exp_neg[:, k, :], gate_inv[:, :], ALU.mult))
            dve.wait_ge(route, step[0])
            for k in range(2):
                routed(dve.tensor_tensor(part[:, k, :, :], chosen[:, k, :, :], over_experts(share[:, k, :]),
                                         ALU.mult))
            dve.wait_ge(route, step[0])
            dve.tensor_tensor(combine[:, :, 0:E], part[:, 0, :, :], part[:, 1, :, :],
                              ALU.add).then_inc(combine_made, 1)
            dve.wait_ge(combine_made, 1)
            dve.sem_inc(combine_made, 1)

            for t in range(T):
                dve.wait_ge(b2_made, t + 1)
                dve.wait_ge(hn_added, t + 1)
                dve.tensor_tensor(acc[:, t, :], bank[4 + t % 4][:, 0:D], acc[:, t, :], ALU.add).then_inc(b2_added, 1)

            def expert(n, j, first):
                e = 2 * n + j
                for h in range(2):
                    dve.wait_ge(up_made, 2 * e + h + 1)
                    dve.wait_ge(gelu_made, 2 * e + h + 1)
                    if not first:
                        dve.wait_ge(down_made, 4 * (e - 1) + 2 * h + 2)
                    dve.scalar_tensor_tensor(out=y_t[:, h, :], in0=bank[2 + h][:, :],
                                             scalar=bias_t[:, bass.ds(EA + col_of(e), 1)], in1=gated[:, h, :],
                                             op0=ALU.add, op1=ALU.mult).then_inc(y_made, 1)
                for t in range(T):
                    if t % 2 == 0:
                        dve.wait_ge(down_made, 4 * e + t // 2 + 1)
                    if first:
                        dve.wait_ge(b2_added, t + 1)
                    else:
                        dve.wait_ge(down_added, 8 * (e - 1) + t + 1)
                    dve.scalar_tensor_tensor(out=acc[:, t, :], in0=bank[4 + t // 2][:, (t % 2) * D:(t % 2 + 1) * D],
                                             scalar=combine[:, t, bass.ds(col_of(e), 1)], in1=acc[:, t, :],
                                             op0=ALU.mult, op1=ALU.add).then_inc(down_added, 1)

            for j in range(SH):
                expert(0, j, j == 0)
            with dve.Fori(1, EA // 2) as n:
                for j in range(2):
                    expert(n, j, False)


_INS = ["x", "ctx_2048", "mask_BxS2_bk0", "L0_ffn_wa", "L0_ffn_rg", "L0_ffn_rgb", "L0_ffn_rw1", "L0_ffn_rb1",
        "L0_ffn_rw2", "L0_ffn_rb2", "L0_ffn_sg", "L0_ffn_sgb", "L0_ffn_sw1", "L0_ffn_sb1", "L0_ffn_sw2",
        "L0_ffn_sb2"]
_OUTS = [((8, 128, 256), "float32")]


def kernel(**inputs):
    import numpy as _np
    import concourse.bacc as _bacc
    from concourse import mybir as _mybir
    from concourse.bass_utils import run_bass_kernel_spmd as _run

    nc = _bacc.Bacc("TRN2", target_bir_lowering=False, num_devices=1)
    arrays, args = {}, []
    for name in _INS:
        a = _np.ascontiguousarray(inputs[name])
        arrays[f"in_{name}_dram"] = a
        args.append(nc.dram_tensor(f"in_{name}_dram", a.shape, _mybir.dt.from_np(a.dtype), kind="ExternalInput").ap())
    for i, (shape, dtype) in enumerate(_OUTS):
        dt = _mybir.dt.from_np(_np.dtype(dtype))
        args.append(nc.dram_tensor(f"out_{i}_dram", shape, dt, kind="ExternalOutput").ap())
    xattn_moe(nc, *args)
    r = _run(nc, [arrays], core_ids=[0])
    got = tuple(r.results[0][f"out_{i}_dram"] for i in range(len(_OUTS)))
    return got[0]
```

```python
from contextlib import ExitStack

import concourse.bass as bass
from concourse import mybir

P = 128
F32 = mybir.dt.float32
U8 = mybir.dt.uint8
I32 = mybir.dt.int32
U32 = mybir.dt.uint32
BF16 = mybir.dt.bfloat16
ALU = mybir.AluOpType
ACT = mybir.ActivationFunctionType
AX = mybir.AxisListType
EPS = 1e-5
NEG = -1e30


def xattn_moe(nc, x, ctx_mem, mask, wa, rg, rgb, rw1, rb1, rw2, rb2, sg, sgb, sw1, sb1, sw2, sb2, out):
    T, S, D = x.shape
    E, _, F = rg.shape
    SH = sg.shape[0]
    EA = E + SH
    KC = D // P
    HALF = T * P // 2
    SCALE = float(D) ** -0.5
    FIRST = 2
    K = 2
    SLOT_READ = 5
    CONSTS = 10
    ROUTED_LOADS = 5 * E // 4 + 2
    ROUTE_BEST = 12
    NT = K * T + E - 1
    RING = 4
    LAST_LAG = 3
    PEELED = 7
    TURNS = (NT - PEELED) // RING
    assert NT == PEELED + RING * TURNS
    assert S == P and F == P and D == 2 * P and SH == 2 and E % 2 == 0

    stack = ExitStack()
    with stack:
        def sb(name, shape, dt=F32):
            return stack.enter_context(nc.sbuf_tensor(name, shape, dt))

        def sem(name):
            return stack.enter_context(nc.semaphore(name))

        bank = [stack.enter_context(nc.psum_tensor(f"bank{i}", [P, 512], F32)) for i in range(8)]

        ident = sb("ident", [P, P])
        power = sb("power", [P, T])
        ones_row = sb("ones_row", [1, P])
        expert_no = sb("expert_no", [P, T, E])
        xs = sb("xs", [P, T, D])
        mem = sb("mem", [P, T, D])
        mask_row = sb("mask_row", [1, T * P], U8)
        wa_sb = sb("wa_sb", [P, KC, E])
        bias_rows = sb("bias_rows", [2 * EA, F])
        b2_rows = sb("b2_rows", [EA, D])
        shut_row = sb("shut_row", [1, T * P])
        any_row = sb("any_row", [1, T])
        any_open = sb("any_open", [P, T])
        stats = sb("stats", [P, T, 6])
        mean_var = sb("mean_var", [P, T, 2])
        var_eps = sb("var_eps", [P, T])
        rstd = sb("rstd", [P, T])
        xn = sb("xn", [P, T, D])
        xm_t = sb("xm_t", [P, T, 4, P])
        row_max = sb("row_max", [P, T])
        neg_max = sb("neg_max", [P, T])
        probs = sb("probs", [P, T, P])
        prob_sum = sb("prob_sum", [P, T])
        prob_inv = sb("prob_inv", [P, T])
        prob_scale = sb("prob_scale", [P, T])
        probs_t = sb("probs_t", [P, T, P])
        acc = sb("acc", [P, T, D])
        stats2 = sb("stats2", [P, T, 6])
        mean_var2 = sb("mean_var2", [P, T, 2])
        var_eps2 = sb("var_eps2", [P, T])
        rstd2 = sb("rstd2", [P, T])
        hn = sb("hn", [P, T, D])
        hn_t = sb("hn_t", [P, KC, T * P])
        logits = sb("logits", [P, T, E])
        hit = sb("hit", [P, T, E])
        place = sb("place", [P, T, E])
        best = sb("best", [P, 2, T])
        best_no = sb("best_no", [P, 2, T])
        chosen = sb("chosen", [P, 2, T, E])
        rest = sb("rest", [P, T, E])
        exp_neg = sb("exp_neg", [P, 2, T])
        one_plus = sb("one_plus", [P, 2, T])
        gate_sum = sb("gate_sum", [P, T])
        gate_inv = sb("gate_inv", [P, T])
        share = sb("share", [P, 2, T])
        part = sb("part", [P, 2, T, E])
        combine = sb("combine", [P, T, EA])
        combine_t = sb("combine_t", [EA, T * P])
        bias_t = sb("bias_t", [P, 2 * EA])
        wg = sb("wg", [P, SH, KC, F])
        wu = sb("wu", [P, SH, KC, F])
        wd = sb("wd", [P, SH, D])
        before = sb("before", [P, P])
        ones = sb("ones", [P, P])
        fill_mark = sb("fill_mark", [P, E, T])
        lower = sb("lower", [P, E, E])
        tile_no = sb("tile_no", [1, NT, E])
        taken = sb("taken", [P, T, E])
        fills = sb("fills", [P, E, T])
        tiles = sb("tiles", [P, E])
        tiles_before = sb("tiles_before", [P, E, E])
        base = sb("base", [P, E])
        end = sb("end", [1, E])
        past = sb("past", [1, NT, E])
        tile_expert_f = sb("tile_expert_f", [1, NT])
        tile_expert = sb("tile_expert", [1, NT], I32)
        slot_of = sb("slot_of", [P, T, E])
        slot_part = sb("slot_part", [P, K, T, E])
        slot_f = sb("slot_f", [P, K, T])
        slot = sb("slot", [P, K, T], U32)
        zeros = sb("zeros", [P, D])
        w_gu = sb("w_gu", [P, KC, E, 2 * F])
        w_d = sb("w_d", [P, E, D])
        bias_gu = sb("bias_gu", [P, E, 2 * F])
        slots_in = sb("slots_in", [P, RING, D])
        slots_t = sb("slots_t", [P, 2, KC, P])
        biased = sb("biased", [P, 2, 2 * F])
        r_gated = sb("r_gated", [P, 2, F])
        r_y = sb("r_y", [P, 2, F])
        r_yt = sb("r_yt", [P, 2, P])
        r_out = sb("r_out", [P, RING, D])
        picked = xm_t[:, :, :, :].rearrange("p t (k c) s -> p k t (c s)", k=K)
        slots_dram = nc.dram_tensor("slots_dram", [NT * P, D], F32).ap()
        expert_out_dram = nc.dram_tensor("expert_out_dram", [NT * P, D], F32).ap()
        gated = sb("gated", [P, 2, HALF])
        y_t = sb("y_t", [P, 2, HALF])

        ident_made = sem("ident_made")
        consts = sem("consts")
        power_made = sem("power_made")
        eps_made = sem("eps_made")
        eps2_made = sem("eps2_made")
        x_in = [sem("x_in0"), sem("x_in1")]
        mem_in = [sem("mem_in0"), sem("mem_in1")]
        mask_in = sem("mask_in")
        small_in = sem("small_in")
        w_in = [sem("w_in0"), sem("w_in1")]
        out_done = sem("out_done")
        shut_made = sem("shut_made")
        any_summed = sem("any_summed")
        any_made = sem("any_made")
        stat_made = sem("stat_made")
        aggr_made = sem("aggr_made")
        rstd_made = sem("rstd_made")
        xn_made = sem("xn_made")
        xm_turned = sem("xm_turned")
        xm_copied = sem("xm_copied")
        scores_made = sem("scores_made")
        max_made = sem("max_made")
        neg_made = sem("neg_made")
        probs_made = sem("probs_made")
        probs_turned = sem("probs_turned")
        probs_copied = sem("probs_copied")
        inv_made = sem("inv_made")
        scale_made = sem("scale_made")
        read_made = sem("read_made")
        h_made = sem("h_made")
        stat2_made = sem("stat2_made")
        aggr2_made = sem("aggr2_made")
        rstd2_made = sem("rstd2_made")
        hn_made = sem("hn_made")
        hn_turned = sem("hn_turned")
        hn_copied = sem("hn_copied")
        logits_made = sem("logits_made")
        route = sem("route")
        gate_exp = sem("gate_exp")
        combine_made = sem("combine_made")
        combine_turned = sem("combine_turned")
        combine_copied = sem("combine_copied")
        bias_turned = sem("bias_turned")
        bias_copied = sem("bias_copied")
        hn_added = sem("hn_added")
        b2_made = sem("b2_made")
        b2_added = sem("b2_added")
        zeros_made = sem("zeros_made")
        slots_cleared = sem("slots_cleared")
        routed_in = sem("routed_in")
        taken_made = sem("taken_made")
        ranks_made = sem("ranks_made")
        slot_step = sem("slot_step")
        slot_made = sem("slot_made")
        tile_expert_made = sem("tile_expert_made")
        slots_sent = sem("slots_sent")
        slots_read = [sem(f"slots_read{j}") for j in range(RING)]
        slots_turned = sem("slots_turned")
        slots_copied = sem("slots_copied")
        r_up_made = sem("r_up_made")
        r_biased = sem("r_biased")
        r_gelu_made = sem("r_gelu_made")
        r_y_made = sem("r_y_made")
        r_y_turned = sem("r_y_turned")
        r_y_copied = sem("r_y_copied")
        r_down_made = sem("r_down_made")
        r_out_copied = sem("r_out_copied")
        r_out_sent = [sem(f"r_out_sent{j}") for j in range(RING)]
        picked_in = [sem(f"picked_in{i}") for i in range(K * T)]
        picked_added = sem("picked_added")
        gate_made = sem("gate_made")
        up_made = sem("up_made")
        gelu_made = sem("gelu_made")
        y_made = sem("y_made")
        down_made = sem("down_made")
        down_added = sem("down_added")

        block = stack.enter_context(nc.Block())

        @block.sync
        def _(sp):
            for g, (a, b) in enumerate(((0, FIRST), (FIRST, T))):
                sp.dma_start(xs[:, a:b, :], x[a:b].rearrange("t p d -> p t d")).then_inc(x_in[g], 16)
                sp.dma_start(mem[:, a:b, :], ctx_mem[a:b].rearrange("t p d -> p t d")).then_inc(mem_in[g], 16)
                if g == 0:
                    sp.dma_start(mask_row[:, :], mask.rearrange("(o t) m -> o (t m)", o=1)).then_inc(mask_in, 16)
            sp.dma_start(wa_sb[:, :, :], wa.rearrange("(c p) e -> p c e", p=P)).then_inc(small_in, 16)
            for row, src in ((0, rgb), (E, sgb), (EA, rb1), (EA + E, sb1)):
                sp.dma_start(bias_rows[row:row + src.shape[0], :], src).then_inc(small_in, 16)
            sp.dma_start(b2_rows[0:E, :], rb2).then_inc(small_in, 16)
            sp.dma_start(b2_rows[E:EA, :], sb2).then_inc(small_in, 16)

            def load_expert(j, g, w1, w2):
                sp.dma_start(wg[:, j, :, :], g.rearrange("o (c p) f -> p (o c) f", p=P)).then_inc(w_in[j], 16)
                sp.dma_start(wu[:, j, :, :], w1.rearrange("o (c p) f -> p (o c) f", p=P)).then_inc(w_in[j], 16)
                sp.dma_start(wd[:, j, :], w2.rearrange("o f d -> f (o d)")).then_inc(w_in[j], 16)

            for j in range(SH):
                load_expert(j, sg[j:j + 1], sw1[j:j + 1], sw2[j:j + 1])
            sp.wait_ge(zeros_made, 1)
            sp.dma_start(slots_dram.rearrange("(i p) d -> p i d", p=P),
                         zeros[:, :].rearrange("p (o d) -> p o d", o=1).broadcast_to([P, NT, D])).then_inc(slots_cleared, 16)
            for e in range(0, E, 4):
                for c in range(KC):
                    sp.dma_start(w_gu[:, c, e:e + 4, 0:F],
                                 rg[e:e + 4, c * P:(c + 1) * P, :].rearrange("e p f -> p e f")).then_inc(routed_in, 16)
                    sp.dma_start(w_gu[:, c, e:e + 4, F:2 * F],
                                 rw1[e:e + 4, c * P:(c + 1) * P, :].rearrange("e p f -> p e f")).then_inc(routed_in, 16)
                sp.dma_start(w_d[:, e:e + 4, :], rw2[e:e + 4].rearrange("e f d -> f e d")).then_inc(routed_in, 16)
            for half, src in enumerate((rgb, rb1)):
                sp.dma_start(bias_gu[:, :, half * F:(half + 1) * F],
                             src.rearrange("(o e) f -> o e f", o=1).broadcast_to([P, E, F])).then_inc(routed_in, 16)

            def read_slots(n, c):
                t = RING * n + c
                sp.dma_start(slots_in[:, c % RING, :],
                             slots_dram[bass.ds(t * P, P), :]).then_inc(slots_read[c % RING], 16)

            def send_out(n, c):
                t = RING * n + c
                sp.wait_ge(r_out_copied, t + 1)
                sp.dma_start(expert_out_dram[bass.ds(t * P, P), :],
                             r_out[:, c % RING, :]).then_inc(r_out_sent[c % RING], 16)

            def step(n, c):
                sp.wait_ge(slots_turned, RING * n + c + 1)
                read_slots(n, c + RING)
                send_out(n, c - LAST_LAG)

            sp.wait_ge(slots_sent, 16 * K * T)
            for c in range(RING):
                read_slots(0, c)
            for c in range(LAST_LAG):
                sp.wait_ge(slots_turned, c + 1)
                read_slots(0, c + RING)
            with sp.Fori(0, (NT - PEELED) // RING) as n:
                for c in range(LAST_LAG, LAST_LAG + RING):
                    step(n, c)
            for c in range(NT - PEELED, NT):
                send_out(0, c)
            for t in range(T):
                sp.wait_ge(picked_added, K * (t + 1))
                sp.dma_start(out[t], acc[:, t, :]).then_inc(out_done, 16)
            sp.wait_ge(out_done, 16 * T)

        @block.gpsimd
        def _(pool):
            pool.memset(zeros[:, :], 0.0).then_inc(zeros_made, 1)
            pool.memset(ident[:, :], 0.0).then_inc(ident_made, 1)
            pool.wait_ge(ident_made, 1)
            pool.affine_select(out=ident[:, :], in_=ident[:, :], compare_op=ALU.not_equal, fill=1.0, base=0,
                               pattern=[[-1, P]], channel_multiplier=1).then_inc(consts, 1)
            pool.memset(ones_row[:, :], 1.0).then_inc(consts, 1)
            pool.iota(expert_no[:, :, :], pattern=[[0, T], [1, E]], base=0, channel_multiplier=0,
                      allow_small_or_imprecise_dtypes=True).then_inc(consts, 1)
            pool.memset(combine[:, :, E:EA], 1.0).then_inc(consts, 1)
            pool.memset(ones[:, :], 1.0).then_inc(consts, 1)
            pool.wait_ge(consts, 5)
            pool.affine_select(out=before[:, :], in_=ones[:, :], compare_op=ALU.is_gt, fill=0.0, base=0,
                               pattern=[[1, P]], channel_multiplier=-1).then_inc(consts, 1)
            pool.iota(fill_mark[:, :, :], pattern=[[0, E], [P, T]], base=0, channel_multiplier=0,
                      allow_small_or_imprecise_dtypes=True).then_inc(consts, 1)
            pool.memset(lower[:, :, :], 1.0).then_inc(consts, 1)
            pool.iota(tile_no[:, :, :], pattern=[[1, NT], [0, E]], base=0, channel_multiplier=0,
                      allow_small_or_imprecise_dtypes=True).then_inc(consts, 1)
            pool.wait_ge(consts, 9)
            pool.affine_select(out=lower[:, :, :], in_=lower[:, :, :], compare_op=ALU.is_gt, fill=0.0, base=0,
                               pattern=[[1, E], [-1, E]], channel_multiplier=0).then_inc(consts, 1)
            pool.memset(power[:, :], -0.5).then_inc(power_made, 1)
            pool.wait_ge(power_made, 1)

            def inverse_deviation(mv, ve, rs, mv_sem, ve_sem, rs_sem, a, b):
                pool.wait_ge(mv_sem, b)
                pool.tensor_scalar(ve[:, a:b], mv[:, a:b, 1], EPS, None, ALU.add).then_inc(ve_sem, 1)
                pool.wait_ge(ve_sem, 1 if a == 0 else 2)
                pool.tensor_tensor(rs[:, a:b], ve[:, a:b], power[:, a:b], ALU.pow).then_inc(rs_sem, 1)

            for a, b in ((0, FIRST), (FIRST, T)):
                inverse_deviation(mean_var, var_eps, rstd, aggr_made, eps_made, rstd_made, a, b)
            inverse_deviation(mean_var2, var_eps2, rstd2, aggr2_made, eps2_made, rstd2_made, 0, T)
            for t in range(T):
                pool.wait_ge(hn_made, t + 1)
                pool.tensor_tensor(acc[:, t, :], acc[:, t, :], hn[:, t, :], ALU.add).then_inc(hn_added, 1)
            pool.wait_ge(slots_cleared, 16)
            pool.wait_ge(slot_made, 1)
            for t in range(T):
                for k in range(K):
                    pool.indirect_dma_start(
                        out=slots_dram[:, :], out_offset=bass.IndirectOffsetOnAxis(ap=slot[:, k, t:t + 1], axis=0),
                        in_=hn[:, t, :], in_offset=None).then_inc(slots_sent, 16)
            for j in range(RING):
                pool.wait_ge(r_out_sent[j], 16 * len(range(j, NT, RING)))
            for t in range(T):
                for k in range(K):
                    pool.indirect_dma_start(
                        out=picked[:, k, t, :], out_offset=None, in_=expert_out_dram[:, :],
                        in_offset=bass.IndirectOffsetOnAxis(ap=slot[:, k, t:t + 1], axis=0)
                    ).then_inc(picked_in[K * t + k], 16)

        @block.tensor
        def _(pe):
            pe.wait_ge(consts, CONSTS)
            pe.wait_ge(shut_made, 2)
            pe.matmul(bank[7][:, 0:T], ones_row[:, :], any_row[:, :], start=True, stop=True).then_inc(any_summed, 1)
            for t in range(T):
                if t == 0:
                    pe.wait_ge(mem_in[0], 16)
                if t == FIRST:
                    pe.wait_ge(mem_in[1], 16)
                if t >= 2:
                    pe.wait_ge(xm_copied, t - 1)
                for c in range(KC):
                    pe.transpose(bank[t % 2][:, (KC + c) * P:(KC + c + 1) * P], mem[:, t, c * P:(c + 1) * P],
                                 ident[:, :])
                pe.wait_ge(xn_made, t + 1)
                for c in range(KC):
                    mm = pe.transpose(bank[t % 2][:, c * P:(c + 1) * P], xn[:, t, c * P:(c + 1) * P], ident[:, :])
                mm.then_inc(xm_turned, 1)
            for t in range(T):
                pe.wait_ge(xm_copied, t + 1)
                if t >= 2:
                    pe.wait_ge(probs_made, t - 1)
                for c in range(KC):
                    pe.matmul(bank[2 + t % 2][:, 0:P], xm_t[:, t, c, :], xm_t[:, t, KC + c, :],
                              start=(c == 0), stop=False)
                pe.matmul(bank[2 + t % 2][:, 0:P], ones_row[:, :], shut_row[:, t * P:(t + 1) * P],
                          start=False, stop=True).then_inc(scores_made, 1)
            for t in range(T):
                pe.wait_ge(probs_made, t + 1)
                if t >= 2:
                    pe.wait_ge(probs_copied, t - 1)
                pe.transpose(bank[4 + t % 2][:, 0:P], probs[:, t, :], ident[:, :]).then_inc(probs_turned, 1)
            pe.wait_ge(any_made, 1)
            for t in range(T):
                pe.wait_ge(probs_copied, t + 1)
                if t >= 2:
                    pe.wait_ge(h_made, t - 1)
                pe.matmul(bank[6 + t % 2][:, 0:D], probs_t[:, t, :], mem[:, t, :],
                          start=True, stop=True).then_inc(read_made, 1)
            pe.wait_ge(small_in, 7 * 16)
            pe.transpose(bank[4][:, 0:2 * EA], bias_rows[:, :], ident[0:2 * EA, 0:2 * EA]).then_inc(bias_turned, 1)
            for t in range(T):
                pe.wait_ge(hn_made, t + 1)
                if t >= 2:
                    pe.wait_ge(hn_copied, t - 1)
                for c in range(KC):
                    mm = pe.transpose(bank[t % 2][:, c * P:(c + 1) * P], hn[:, t, c * P:(c + 1) * P], ident[:, :])
                mm.then_inc(hn_turned, 1)
            for t in range(T):
                pe.wait_ge(hn_copied, t + 1)
                for c in range(KC):
                    mm = pe.matmul(bank[6][:, t * E:(t + 1) * E], hn_t[:, c, t * P:(t + 1) * P], wa_sb[:, c, :],
                                   start=(c == 0), stop=(c == KC - 1))
            mm.then_inc(logits_made, 1)
            def combine_biases():
                pe.wait_ge(combine_made, 2)
                for t in range(T):
                    mm = pe.transpose(bank[4 + t // 4][0:EA, (t % 4) * P:(t % 4 + 1) * P], combine[:, t, :],
                                      ident[:, :])
                mm.then_inc(combine_turned, 1)
                pe.wait_ge(combine_copied, 2)
                for t in range(T):
                    if t >= 4:
                        pe.wait_ge(b2_added, t - 3)
                    pe.matmul(bank[4 + t % 4][:, 0:D], combine_t[:, t * P:(t + 1) * P], b2_rows[:, :],
                              start=True, stop=True).then_inc(b2_made, 1)

            def ranks():
                pe.wait_ge(taken_made, 1)
                pe.matmul(bank[7][:, 0:T * E], before[:, :], taken[:, :, :], start=True, stop=False,
                          skip_group_check=True)
                for t in range(T):
                    mm = pe.matmul(bank[7][:, (t + 1) * E:(T + 1) * E], ones[:, :],
                                   taken[:, t:t + 1, :].broadcast_to([P, T - t, E]),
                                   start=False, stop=(t == T - 1), skip_group_check=True)
                mm.then_inc(ranks_made, 1)

            def shared_up(e, h):
                if e:
                    pe.wait_ge(gelu_made, 2 * (e - 1) + h + 1)
                for c in range(KC):
                    mm = pe.matmul(bank[h][:, :], wg[:, e, c, :], hn_t[:, c, h * HALF:(h + 1) * HALF],
                                   start=(c == 0), stop=(c == KC - 1))
                mm.then_inc(gate_made, 1)
                if e:
                    pe.wait_ge(y_made, 2 * (e - 1) + h + 1)
                for c in range(KC):
                    mm = pe.matmul(bank[2 + h][:, :], wu[:, e, c, :], hn_t[:, c, h * HALF:(h + 1) * HALF],
                                   start=(c == 0), stop=(c == KC - 1))
                mm.then_inc(up_made, 1)

            def shared_down(e):
                for t in range(T):
                    q, r = t // (T // 2), t % (T // 2)
                    if r == 0:
                        pe.wait_ge(y_made, 2 * e + q + 1)
                    if t % 2 == 0:
                        if e == 0:
                            pe.wait_ge(b2_added, T)
                        else:
                            pe.wait_ge(down_added, 8 * (e - 1) + t + 2)
                    mm = pe.matmul(bank[4 + t // 2][:, (t % 2) * D:(t % 2 + 1) * D],
                                   y_t[:, q, r * P:(r + 1) * P], wd[:, e, :], start=True, stop=True)
                    if t % 2:
                        mm.then_inc(down_made, 1)

            pe.wait_ge(w_in[0], 48)
            shared_up(0, 0)
            ranks()
            shared_up(0, 1)
            pe.wait_ge(bias_copied, 1)
            pe.wait_ge(slot_step, SLOT_READ)
            combine_biases()
            shared_down(0)
            pe.wait_ge(w_in[1], 48)
            shared_up(1, 0)
            shared_up(1, 1)
            shared_down(1)

            def turn_slots(n, c):
                t = RING * n + c
                pe.wait_ge(slots_read[c % RING], 16 * (n + c // RING + 1))
                if isinstance(t, int) and t < 2:
                    pe.wait_ge(gelu_made, 2 * SH)
                else:
                    pe.wait_ge(slots_copied, t - 1)
                for k in range(KC):
                    mm = pe.transpose(bank[c % 2][:, k * P:(k + 1) * P], slots_in[:, c % RING, k * P:(k + 1) * P],
                                      ident[:, :])
                mm.then_inc(slots_turned, 1)

            def routed_up(n, c, e):
                t = RING * n + c
                pe.wait_ge(slots_copied, t + 1)
                if isinstance(t, int) and t < 2:
                    pe.wait_ge(y_made, 2 * SH)
                else:
                    pe.wait_ge(r_biased, t - 1)
                for k in range(KC):
                    mm = pe.matmul(bank[2 + c % 2][:, 0:2 * F], slots_t[:, c % 2, k, :],
                                   w_gu[:, k, bass.ds(e, 1), :], start=(k == 0), stop=(k == KC - 1))
                mm.then_inc(r_up_made, 1)

            def routed_down(n, c, e):
                t = RING * n + c
                pe.wait_ge(r_y_copied, t + 1)
                if isinstance(t, int) and t < 2:
                    pe.wait_ge(down_added, T * SH)
                else:
                    pe.wait_ge(r_out_copied, t - 1)
                pe.matmul(bank[6 + c % 2][:, 0:D], r_yt[:, c % 2, :], w_d[:, bass.ds(e, 1), :],
                          start=True, stop=True).then_inc(r_down_made, 1)

            def turn_y(n, c):
                t = RING * n + c
                pe.wait_ge(r_y_made, t + 1)
                if isinstance(t, int) and t < 2:
                    pe.wait_ge(down_added, T * SH)
                else:
                    pe.wait_ge(r_y_copied, t - 1)
                pe.transpose(bank[4 + c % 2][:, 0:P], r_y[:, c % 2, :], ident[:, :]).then_inc(r_y_turned, 1)

            def expert_of(n, c):
                return pe.value_load(tile_expert[0:1, bass.ds(RING * n + c, 1)], min_val=0, max_val=E - 1)

            def step(n, c):
                s = c if isinstance(n, int) else None
                if s is None or s < NT:
                    turn_slots(n, c)
                if s is None or 1 <= s < NT + 1:
                    routed_up(n, c - 1, expert_of(n, c - 1))
                if s is None or s >= LAST_LAG:
                    routed_down(n, c - LAST_LAG, expert_of(n, c - LAST_LAG))
                if s is None or 2 <= s < NT + 2:
                    turn_y(n, c - 2)

            pe.wait_ge(tile_expert_made, 1)
            pe.wait_ge(routed_in, 16 * ROUTED_LOADS)
            for c in range(PEELED):
                step(0, c)
            with pe.Fori(0, TURNS) as n:
                for c in range(PEELED, PEELED + RING):
                    step(n, c)
            for c in range(NT, NT + LAST_LAG):
                step(0, c)

        def each_tile(step, first=0, last=T):
            for t in range(first, last):
                step(t, t % 2)

        @block.scalar
        def _(act):
            def copy_inputs(t, j):
                act.wait_ge(xm_turned, t + 1)
                act.copy(xm_t[:, t, :, :], bank[j][:, :]).then_inc(xm_copied, 1)
            each_tile(copy_inputs)

            def exp_scores(t, j):
                act.wait_ge(neg_made, t + 1)
                act.activation(probs[:, t, :], bank[2 + j][:, 0:P], ACT.Exp,
                               bias=neg_max[:, t:t + 1], scale=SCALE,
                               accum_out=prob_sum[:, t:t + 1]).then_inc(probs_made, 1)
            each_tile(exp_scores)

            def copy_probs(t, j):
                act.wait_ge(probs_turned, t + 1)
                act.copy(probs_t[:, t, :], bank[4 + j][:, 0:P]).then_inc(probs_copied, 1)
            each_tile(copy_probs)

            act.wait_ge(bias_turned, 1)
            act.copy(bias_t[:, :], bank[4][:, 0:2 * EA]).then_inc(bias_copied, 1)

            def copy_hn(t, j):
                act.wait_ge(hn_turned, t + 1)
                act.copy(hn_t[:, :, t * P:(t + 1) * P],
                         bank[j][:, 0:D].rearrange("p (c s) -> p c s", c=KC)).then_inc(hn_copied, 1)
            each_tile(copy_hn)

            act.wait_ge(route, ROUTE_BEST)
            act.activation(exp_neg[:, :, :], best[:, :, :], ACT.Exp, scale=-1.0).then_inc(gate_exp, 1)
            act.wait_ge(combine_turned, 1)
            for q in range(2):
                act.copy(combine_t[:, q * HALF:(q + 1) * HALF], bank[4 + q][0:EA, :]).then_inc(combine_copied, 1)

            for e in range(SH):
                for h in range(2):
                    act.wait_ge(gate_made, 2 * e + h + 1)
                    if e:
                        act.wait_ge(y_made, 2 * (e - 1) + h + 1)
                    act.activation(gated[:, h, :], bank[h][:, :], ACT.Gelu,
                                   bias=bias_t[:, E + e:E + e + 1]).then_inc(gelu_made, 1)

            def copy_slots(n, c):
                t = RING * n + c
                act.wait_ge(slots_turned, t + 1)
                if not isinstance(t, int) or t >= 2:
                    act.wait_ge(r_up_made, t - 1)
                act.copy(slots_t[:, c % 2, :, :], bank[c % 2][:, 0:D]).then_inc(slots_copied, 1)

            def routed_gelu(n, c):
                t = RING * n + c
                act.wait_ge(r_biased, t + 1)
                if not isinstance(t, int) or t >= 2:
                    act.wait_ge(r_y_made, t - 1)
                act.activation(r_gated[:, c % 2, :], biased[:, c % 2, 0:F], ACT.Gelu).then_inc(r_gelu_made, 1)

            def copy_out(n, c):
                t = RING * n + c
                act.wait_ge(r_down_made, t + 1)
                if not isinstance(t, int) or t >= RING:
                    act.wait_ge(r_out_sent[c % RING], 16 * (n + c // RING))
                act.copy(r_out[:, c % RING, :], bank[6 + c % 2][:, 0:D]).then_inc(r_out_copied, 1)

            def step(n, c):
                s = c if isinstance(n, int) else None
                if s is None or s < NT:
                    copy_slots(n, c)
                if s is None or 1 <= s < NT + 1:
                    routed_gelu(n, c - 1)
                if s is None or s >= LAST_LAG:
                    copy_out(n, c - LAST_LAG)

            for c in range(PEELED):
                step(0, c)
            with act.Fori(0, TURNS) as n:
                for c in range(PEELED, PEELED + RING):
                    step(n, c)
            for c in range(NT, NT + LAST_LAG):
                step(0, c)

        @block.vector
        def _(dve):
            dve.wait_ge(mask_in, 16)
            dve.tensor_scalar(shut_row[:, :], mask_row[:, :], -NEG / SCALE, NEG / SCALE,
                              ALU.mult, ALU.add).then_inc(shut_made, 1)
            dve.tensor_reduce(any_row[:, :], mask_row[:, :].rearrange("o (t m) -> o t m", t=T), AX.X,
                              ALU.max).then_inc(shut_made, 1)

            def layernorm(src, st, mv, rs, dst, st_sem, mv_sem, rs_sem, dst_sem, a, b, before=None):
                def moments(t, j):
                    if before is not None:
                        before(t, j)
                    dve.bn_stats(st[:, t, :], src[:, t, :]).then_inc(st_sem, 1)
                    dve.wait_ge(st_sem, t + 1)
                    dve.bn_aggr(mv[:, t, :], st[:, t, :]).then_inc(mv_sem, 1)
                each_tile(moments, a, b)
                dve.wait_ge(rs_sem, 1 if a == 0 else 2)

                def normalise(t, j):
                    dve.tensor_scalar(dst[:, t, :], src[:, t, :],
                                      mv[:, t, 0:1], rs[:, t:t + 1],
                                      ALU.subtract, ALU.mult).then_inc(dst_sem, 1)
                each_tile(normalise, a, b)

            for g, (a, b) in enumerate(((0, FIRST), (FIRST, T))):
                dve.wait_ge(x_in[g], 16)
                layernorm(xs, stats, mean_var, rstd, xn, stat_made, aggr_made, rstd_made, xn_made, a, b)
            dve.wait_ge(any_summed, 1)
            dve.tensor_copy(any_open[:, :], bank[7][:, 0:T]).then_inc(any_made, 1)

            def maxima(t, j):
                dve.wait_ge(scores_made, t + 1)
                dve.tensor_reduce(row_max[:, t:t + 1], bank[2 + j][:, 0:P], AX.X, ALU.max).then_inc(max_made, 1)
                dve.wait_ge(max_made, t + 1)
                dve.tensor_scalar(neg_max[:, t:t + 1], row_max[:, t:t + 1], -SCALE, None,
                                  ALU.mult).then_inc(neg_made, 1)
            each_tile(maxima)

            dve.wait_ge(probs_made, T)
            dve.reciprocal(prob_inv[:, :], prob_sum[:, :]).then_inc(inv_made, 1)
            dve.wait_ge(inv_made, 1)
            dve.wait_ge(any_made, 1)
            dve.tensor_tensor(prob_scale[:, :], prob_inv[:, :], any_open[:, :], ALU.mult).then_inc(scale_made, 1)
            dve.wait_ge(scale_made, 1)

            def add_readout(t, j):
                dve.wait_ge(read_made, t + 1)
                dve.scalar_tensor_tensor(out=acc[:, t, :], in0=bank[6 + j][:, 0:D],
                                         scalar=prob_scale[:, t:t + 1], in1=xs[:, t, :],
                                         op0=ALU.mult, op1=ALU.add).then_inc(h_made, 1)
                dve.wait_ge(h_made, t + 1)
            layernorm(acc, stats2, mean_var2, rstd2, hn, stat2_made, aggr2_made, rstd2_made, hn_made, 0, T,
                      before=add_readout)

            step = [0]

            def routed(ins):
                step[0] += 1
                ins.then_inc(route, 1)

            def over_experts(v):
                return v.rearrange("p (t o) -> p t o", o=1).broadcast_to([P, T, E])

            dve.wait_ge(consts, CONSTS)
            dve.wait_ge(logits_made, 1)
            routed(dve.tensor_copy(logits[:, :, :], bank[6][:, 0:T * E]))
            dve.wait_ge(route, 1)
            for k in range(2):
                src = logits if k == 0 else rest
                routed(dve.tensor_reduce(best[:, k, :], src[:, :, :], AX.X, ALU.max))
                dve.wait_ge(route, step[0])
                routed(dve.tensor_tensor(hit[:, :, :], src[:, :, :], over_experts(best[:, k, :]), ALU.is_lt))
                dve.wait_ge(route, step[0])
                routed(dve.scalar_tensor_tensor(out=place[:, :, :], in0=hit[:, :, :], scalar=float(E),
                                                in1=expert_no[:, :, :], op0=ALU.mult, op1=ALU.add))
                dve.wait_ge(route, step[0])
                routed(dve.tensor_reduce(best_no[:, k, :], place[:, :, :], AX.X, ALU.min))
                dve.wait_ge(route, step[0])
                routed(dve.tensor_tensor(chosen[:, k, :, :], expert_no[:, :, :], over_experts(best_no[:, k, :]),
                                         ALU.is_equal))
                dve.wait_ge(route, step[0])
                if k == 0:
                    routed(dve.scalar_tensor_tensor(out=rest[:, :, :], in0=chosen[:, 0, :, :], scalar=-3e38,
                                                    in1=logits[:, :, :], op0=ALU.mult, op1=ALU.add))
                    dve.wait_ge(route, step[0])
            assert step[0] == ROUTE_BEST
            dve.wait_ge(consts, CONSTS)
            dve.tensor_tensor(taken[:, :, :], chosen[:, 0, :, :], chosen[:, 1, :, :], ALU.add).then_inc(taken_made, 1)
            dve.wait_ge(gate_exp, 1)
            routed(dve.tensor_scalar(one_plus[:, :, :], exp_neg[:, :, :], 1.0, None, ALU.add))
            dve.wait_ge(route, step[0])
            routed(dve.reciprocal(exp_neg[:, :, :], one_plus[:, :, :]))
            dve.wait_ge(route, step[0])
            routed(dve.tensor_tensor(gate_sum[:, :], exp_neg[:, 0, :], exp_neg[:, 1, :], ALU.add))
            dve.wait_ge(route, step[0])
            routed(dve.reciprocal(gate_inv[:, :], gate_sum[:, :]))
            dve.wait_ge(route, step[0])
            for k in range(2):
                routed(dve.tensor_tensor(share[:, k, :], exp_neg[:, k, :], gate_inv[:, :], ALU.mult))
            dve.wait_ge(route, step[0])
            for k in range(2):
                routed(dve.tensor_tensor(part[:, k, :, :], chosen[:, k, :, :], over_experts(share[:, k, :]),
                                         ALU.mult))
            dve.wait_ge(route, step[0])
            dve.tensor_tensor(combine[:, :, 0:E], part[:, 0, :, :], part[:, 1, :, :],
                              ALU.add).then_inc(combine_made, 1)
            dve.wait_ge(combine_made, 1)
            dve.sem_inc(combine_made, 1)

            done = [0]

            def slotted(ins):
                done[0] += 1
                ins.then_inc(slot_step, 1)
                dve.wait_ge(slot_step, done[0])

            dve.wait_ge(ranks_made, 1)
            counts = bank[7][:, T * E:(T + 1) * E]
            slotted(dve.tensor_tensor(fills[:, :, :], counts.rearrange("p (e o) -> p e o", o=1).broadcast_to([P, E, T]),
                                      fill_mark[:, :, :], ALU.is_gt))
            slotted(dve.tensor_reduce(tiles[:, :], fills[:, :, :], AX.X, ALU.add))
            slotted(dve.tensor_tensor(tiles_before[:, :, :], lower[:, :, :],
                                      tiles[:, :].rearrange("p (o f) -> p o f", o=1).broadcast_to([P, E, E]), ALU.mult))
            slotted(dve.tensor_reduce(base[:, :], tiles_before[:, :, :], AX.X, ALU.add))
            slotted(dve.scalar_tensor_tensor(out=slot_of[:, :, :],
                                             in0=base[:, :].rearrange("p (o e) -> p o e", o=1).broadcast_to([P, T, E]),
                                             scalar=float(P), in1=bank[7][:, 0:T * E].rearrange("p (t e) -> p t e", t=T),
                                             op0=ALU.mult, op1=ALU.add))
            assert done[0] == SLOT_READ
            for k in range(K):
                slotted(dve.tensor_tensor(slot_part[:, k, :, :], chosen[:, k, :, :], slot_of[:, :, :], ALU.mult))
            slotted(dve.tensor_reduce(slot_f[:, :, :], slot_part[:, :, :, :], AX.X, ALU.add))
            dve.tensor_copy(slot[:, :, :], slot_f[:, :, :]).then_inc(slot_made, 1)
            slotted(dve.tensor_tensor(end[:, :], base[0:1, :], tiles[0:1, :], ALU.add))
            slotted(dve.tensor_tensor(past[:, :, :], end[:, :].rearrange("p (o e) -> p o e", o=1).broadcast_to([1, NT, E]),
                                      tile_no[:, :, :], ALU.is_le))
            slotted(dve.tensor_reduce(tile_expert_f[:, :], past[:, :, :], AX.X, ALU.add))
            dve.tensor_scalar(tile_expert[:, :], tile_expert_f[:, :], float(E - 1), None,
                              ALU.min).then_inc(tile_expert_made, 1)

            for t in range(T):
                dve.wait_ge(b2_made, t + 1)
                dve.wait_ge(hn_added, t + 1)
                dve.tensor_tensor(acc[:, t, :], bank[4 + t % 4][:, 0:D], acc[:, t, :], ALU.add).then_inc(b2_added, 1)

            for e in range(SH):
                for h in range(2):
                    dve.wait_ge(up_made, 2 * e + h + 1)
                    dve.wait_ge(gelu_made, 2 * e + h + 1)
                    if e:
                        dve.wait_ge(down_made, 4 * (e - 1) + 2 * h + 2)
                    dve.scalar_tensor_tensor(out=y_t[:, h, :], in0=bank[2 + h][:, :],
                                             scalar=bias_t[:, EA + E + e:EA + E + e + 1], in1=gated[:, h, :],
                                             op0=ALU.add, op1=ALU.mult).then_inc(y_made, 1)
                for t in range(T):
                    if t % 2 == 0:
                        dve.wait_ge(down_made, 4 * e + t // 2 + 1)
                    if e == 0:
                        dve.wait_ge(b2_added, t + 1)
                    else:
                        dve.wait_ge(down_added, 8 * (e - 1) + t + 1)
                    dve.tensor_tensor(acc[:, t, :], bank[4 + t // 2][:, (t % 2) * D:(t % 2 + 1) * D], acc[:, t, :],
                                      ALU.add).then_inc(down_added, 1)

            def add_bias(n, c, e):
                t = RING * n + c
                dve.wait_ge(r_up_made, t + 1)
                if not isinstance(t, int) or t >= 2:
                    dve.wait_ge(r_y_made, t - 1)
                dve.tensor_tensor(biased[:, c % 2, :], bank[2 + c % 2][:, 0:2 * F],
                                  bias_gu[:, bass.ds(e, 1), :].rearrange("p o f -> p (o f)"), ALU.add).then_inc(r_biased, 1)

            def multiply(n, c):
                t = RING * n + c
                dve.wait_ge(r_biased, t + 1)
                dve.wait_ge(r_gelu_made, t + 1)
                if not isinstance(t, int) or t >= 2:
                    dve.wait_ge(r_y_turned, t - 1)
                dve.tensor_tensor(r_y[:, c % 2, :], r_gated[:, c % 2, :], biased[:, c % 2, F:2 * F],
                                  ALU.mult).then_inc(r_y_made, 1)

            def copy_y(n, c):
                t = RING * n + c
                dve.wait_ge(r_y_turned, t + 1)
                if not isinstance(t, int) or t >= 2:
                    dve.wait_ge(r_down_made, t - 1)
                dve.tensor_copy(r_yt[:, c % 2, :], bank[4 + c % 2][:, 0:P]).then_inc(r_y_copied, 1)

            def step(n, c):
                s = c if isinstance(n, int) else None
                if s is None or 1 <= s < NT + 1:
                    e = dve.value_load(tile_expert[0:1, bass.ds(RING * n + c - 1, 1)], min_val=0, max_val=E - 1)
                    add_bias(n, c - 1, e)
                    multiply(n, c - 1)
                if s is None or 2 <= s < NT + 2:
                    copy_y(n, c - 2)

            dve.wait_ge(tile_expert_made, 1)
            dve.wait_ge(routed_in, 16 * ROUTED_LOADS)
            for c in range(PEELED):
                step(0, c)
            with dve.Fori(0, TURNS) as n:
                for c in range(PEELED, PEELED + RING):
                    step(n, c)
            for c in range(NT, NT + LAST_LAG):
                step(0, c)

            for t in range(T):
                for k in range(K):
                    dve.wait_ge(picked_in[K * t + k], 16)
                    if k == 0:
                        dve.wait_ge(down_added, T * (SH - 1) + t + 1)
                    else:
                        dve.wait_ge(picked_added, K * t + k)
                    dve.scalar_tensor_tensor(out=acc[:, t, :], in0=picked[:, k, t, :], scalar=share[:, k, t:t + 1],
                                             in1=acc[:, t, :], op0=ALU.mult, op1=ALU.add).then_inc(picked_added, 1)


_INS = ["x", "ctx_2048", "mask_BxS2_bk0", "L0_ffn_wa", "L0_ffn_rg", "L0_ffn_rgb", "L0_ffn_rw1", "L0_ffn_rb1",
        "L0_ffn_rw2", "L0_ffn_rb2", "L0_ffn_sg", "L0_ffn_sgb", "L0_ffn_sw1", "L0_ffn_sb1", "L0_ffn_sw2",
        "L0_ffn_sb2"]
_OUTS = [((8, 128, 256), "float32")]


def kernel(**inputs):
    import numpy as _np
    import concourse.bacc as _bacc
    from concourse import mybir as _mybir
    from concourse.bass_utils import run_bass_kernel_spmd as _run

    nc = _bacc.Bacc("TRN2", target_bir_lowering=False, num_devices=1)
    arrays, args = {}, []
    for name in _INS:
        a = _np.ascontiguousarray(inputs[name])
        arrays[f"in_{name}_dram"] = a
        args.append(nc.dram_tensor(f"in_{name}_dram", a.shape, _mybir.dt.from_np(a.dtype), kind="ExternalInput").ap())
    for i, (shape, dtype) in enumerate(_OUTS):
        dt = _mybir.dt.from_np(_np.dtype(dtype))
        args.append(nc.dram_tensor(f"out_{i}_dram", shape, dt, kind="ExternalOutput").ap())
    xattn_moe(nc, *args)
    r = _run(nc, [arrays], core_ids=[0])
    got = tuple(r.results[0][f"out_{i}_dram"] for i in range(len(_OUTS)))
    return got[0]
```

```python
from contextlib import ExitStack

import concourse.bass as bass
from concourse import mybir

P = 128
F32 = mybir.dt.float32
U8 = mybir.dt.uint8
I32 = mybir.dt.int32
U32 = mybir.dt.uint32
BF16 = mybir.dt.bfloat16
ALU = mybir.AluOpType
ACT = mybir.ActivationFunctionType
AX = mybir.AxisListType
PE = mybir.EngineType.PE
DVE = mybir.EngineType.DVE
EPS = 1e-5
NEG = -1e30


def xattn_moe(nc, x, ctx_mem, mask, wa, rg, rgb, rw1, rb1, rw2, rb2, sg, sgb, sw1, sb1, sw2, sb2, out):
    T, S, D = x.shape
    E, _, F = rg.shape
    SH = sg.shape[0]
    EA = E + SH
    K = 2
    KC = D // P
    HALF = T * P // 2
    SCALE = float(D) ** -0.5
    assert S == P and F == P and D == 2 * P and SH == 2 and E % 4 == 0 and T == 8

    NT = K * T + E - 1
    TILE_NOS = -(-NT // 4) * 4
    LAST_LAG = 3
    PEELED = 7
    UNROLL = 12
    TURNS = (NT - PEELED) // UNROLL
    RING = 4
    SLOT_RING = 6
    assert NT == PEELED + UNROLL * TURNS and UNROLL % RING == 0 and UNROLL % SLOT_RING == 0

    GROUPS = ((0, 2), (2, 5), (5, T))
    PROBS_COPIED_BY = ((0, 2, 4, 5, 6, 7), (1, 3))
    ROUTED_TOGETHER = ((0, 4), (4, 6), (6, T))
    SENT_TOGETHER = 4
    ROUTED_LOADS = 5 * E // 4 + 4
    CONSTS = 6
    RANKS_READ = 10

    XM_BANK = (0, 1, 7, 6)
    PROBS_BANK = (0, 1, 7)
    HN_BANK = (0, 1, 7)
    GATE_BANK = ((5, 1), (0, 2))
    UP_BANK = ((6, 3), (5, 1))
    DOWN_BANK = (2, 3, 4, 7)
    TURNED_BANK = (4, 7)

    stack = ExitStack()
    with stack:
        def sb(name, shape, dt=F32):
            return stack.enter_context(nc.sbuf_tensor(name, shape, dt))

        def sem(name):
            return stack.enter_context(nc.semaphore(name))

        bank = [stack.enter_context(nc.psum_tensor(f"bank{i}", [P, 512], F32)) for i in range(8)]

        ident = sb("ident", [P, P])
        power = sb("power", [P, T])
        ones_row = sb("ones_row", [1, P], BF16)
        zeros = sb("zeros", [P, P])
        expert_no = sb("expert_no", [P, T, E])
        xs = sb("xs", [P, T, D])
        mem = sb("mem", [P, T, D])
        mask_row = sb("mask_row", [1, T * P], U8)
        wa_sb = sb("wa_sb", [P, KC, E])
        bias_rows = sb("bias_rows", [2 * EA, F])
        b2_rows = sb("b2_rows", [EA, D])
        shut_row = sb("shut_row", [1, T * P], BF16)
        stats = sb("stats", [P, T, 6])
        mean_var = sb("mean_var", [P, T, 2])
        var_eps = sb("var_eps", [P, T])
        exp_scale = sb("exp_scale", [P, T])
        neg_scale = sb("neg_scale", [P, T])
        rows = sb("rows", [P, K, T, D + 2])
        share = rows[:, :, :, D + 1:D + 2]
        hn = rows[:, 0, :, 0:D]
        rows_dest = rows[:, :, :, :].bitcast(U32)[:, :, :, D:D + 1]
        xc = rows[:, 1, :, 0:D]
        xm_t = sb("xm_t", [P, T, 4, P])
        row_max = sb("row_max", [P, T])
        neg_max = sb("neg_max", [P, T])
        probs = sb("probs", [P, T, P])
        prob_sum = sb("prob_sum", [P, T])
        prob_inv = sb("prob_inv", [P, T])
        prob_scale = sb("prob_scale", [P, T])
        probs_t = sb("probs_t", [P, T, P])
        acc = sb("acc", [P, T, D])
        stats2 = sb("stats2", [P, T, 6])
        mean_var2 = sb("mean_var2", [P, T, 2])
        var_eps2 = sb("var_eps2", [P, T])
        rstd2 = sb("rstd2", [P, T])
        shift2 = sb("shift2", [P, T])
        hn_t = sb("hn_t", [P, KC, T * P])
        best = sb("best", [P, T, 8])
        best_no = sb("best_no", [P, T, 8], U32)
        chosen = sb("chosen", [P, K, T, E])
        exp_neg = sb("exp_neg", [P, 2, T])
        one_plus = sb("one_plus", [P, 2, T])
        gate_sum = sb("gate_sum", [P, T])
        gate_inv = sb("gate_inv", [P, T])
        part = sb("part", [P, 2, T, E])
        combine = sb("combine", [P, T, EA])
        combine_t = sb("combine_t", [EA, T * P])
        bias_t = sb("bias_t", [P, 2 * EA])
        wg = sb("wg", [P, SH, KC, F])
        wu = sb("wu", [P, SH, KC, F])
        wd = sb("wd", [P, SH, D])
        before = sb("before", [P, P], BF16)
        ones = sb("ones", [P, P], BF16)
        fill_mark = sb("fill_mark", [P, E, T])
        tile_no = sb("tile_no", [1, TILE_NOS, E])
        taken = sb("taken", [P, T, E], BF16)
        fills = sb("fills", [P, E, T])
        tiles = sb("tiles", [P, E])
        end = sb("end", [P, E])
        rank_from_end = sb("rank_from_end", [P, T, E])
        past = sb("past", [1, TILE_NOS, E])
        tile_expert_f = sb("tile_expert_f", [1, TILE_NOS])
        tile_expert = sb("tile_expert", [1, TILE_NOS], I32)
        slot_of = sb("slot_of", [P, T, E])
        slot_part = sb("slot_part", [P, K, T, E])
        slot = sb("slot", [P, K, T], U32)
        empty = sb("empty", [P, D + 2])
        dest = sb("dest", [P, RING], U32)
        w_gu = sb("w_gu", [P, KC, E, 2 * F])
        w_d = sb("w_d", [P, E, D])
        bias_gu = sb("bias_gu", [P, E, 2 * F])
        slots_in = sb("slots_in", [P, SLOT_RING, D + 2])
        slots_t = sb("slots_t", [P, 2, KC, P])
        biased = sb("biased", [P, 2, 2 * F])
        r_gated = sb("r_gated", [P, 2, F])
        r_y = sb("r_y", [P, 2, F])
        r_yt = sb("r_yt", [P, 2, P])
        r_out = sb("r_out", [P, RING, D])
        picked = xm_t[:, :, :, :].rearrange("p t (k c) s -> p k t (c s)", k=K)
        slots_dram = nc.dram_tensor("slots_dram", [NT * P, D + 2], F32).ap()
        results_dram = nc.dram_tensor("results_dram", [K * T * P, D], F32).ap()
        gated = sb("gated", [P, 2, HALF])
        y_t = sb("y_t", [P, 2, HALF])

        ident_made = sem("ident_made")
        ones_made = sem("ones_made")
        zeros_made = sem("zeros_made")
        consts = sem("consts")
        power_made = sem("power_made")
        eps_made = sem("eps_made")
        eps2_made = sem("eps2_made")
        x_in = [sem(f"x_in{g}") for g in range(len(GROUPS))]
        mem_in = [sem(f"mem_in{g}") for g in range(len(GROUPS))]
        mask_in = sem("mask_in")
        small_in = sem("small_in")
        w_in = [sem("w_in0"), sem("w_in1")]
        out_done = sem("out_done")
        shut_made = sem("shut_made")
        stat_made = sem("stat_made")
        aggr_made = sem("aggr_made")
        xc_made = sem("xc_made")
        scale1_made = sem("scale1_made")
        scale1_negated = sem("scale1_negated")
        sum_bounded = sem("sum_bounded")
        xm_turned = sem("xm_turned")
        xm_copied = sem("xm_copied")
        scores_made = sem("scores_made")
        max_made = sem("max_made")
        neg_made = sem("neg_made")
        probs_made = sem("probs_made")
        probs_turned = sem("probs_turned")
        probs_copied = [sem("probs_copied_by_act"), sem("probs_copied_by_dve")]
        inv_made = sem("inv_made")
        scale_made = sem("scale_made")
        read_made = sem("read_made")
        h_made = sem("h_made")
        stat2_made = sem("stat2_made")
        aggr2_made = sem("aggr2_made")
        rstd2_made = sem("rstd2_made")
        shift2_made = sem("shift2_made")
        hn_made = [sem("hn_made_even"), sem("hn_made_odd")]
        hn_turned = sem("hn_turned")
        hn_copied = sem("hn_copied")
        logits_made = sem("logits_made")
        best_made = sem("best_made")
        best_no_made = sem("best_no_made")
        route = sem("route")
        gate_exp = sem("gate_exp")
        combine_made = sem("combine_made")
        combine_turned = sem("combine_turned")
        combine_copied = sem("combine_copied")
        bias_turned = sem("bias_turned")
        bias_copied = sem("bias_copied")
        hn_added = sem("hn_added")
        empty_made = sem("empty_made")
        dest_copied = sem("dest_copied")
        pool_waited = sem("pool_waited")
        rows_made = sem("rows_made")
        share_made = sem("share_made")
        slots_cleared = sem("slots_cleared")
        routed_in = sem("routed_in")
        taken_made = sem("taken_made")
        ranks_made = sem("ranks_made")
        slot_made = sem("slot_made")
        tile_expert_made = sem("tile_expert_made")
        slots_sent = [sem(f"slots_sent{i}") for i in range(K * T // SENT_TOGETHER)]
        slots_read = [sem(f"slots_read{j}") for j in range(SLOT_RING)]
        slots_turned = sem("slots_turned")
        slots_copied = sem("slots_copied")
        r_up_made = sem("r_up_made")
        r_biased = sem("r_biased")
        r_gelu_made = sem("r_gelu_made")
        r_y_made = sem("r_y_made")
        r_y_turned = sem("r_y_turned")
        r_y_copied = sem("r_y_copied")
        r_down_made = sem("r_down_made")
        r_out_copied = sem("r_out_copied")
        r_out_sent = [sem(f"r_out_sent{j}") for j in range(RING)]
        picked_in = [[sem(f"picked_in{t}_{k}") for k in range(K)] for t in range(0, T, 2)]
        picked_added = sem("picked_added")
        gate_made = sem("gate_made")
        up_made = sem("up_made")
        gelu_made = sem("gelu_made")
        y_made = sem("y_made")
        first_down_made = sem("first_down_made")
        shared_made = sem("shared_made")
        down_added = sem("down_added")

        block = stack.enter_context(nc.Block())

        def experts_of(engine, n, a, b):
            a, b = a // 4 * 4, -(-b // 4) * 4
            _, values = nc.values_load_multi_w_load_instructions(
                tile_expert[0:1, bass.ds(UNROLL * n + a, b - a)], engines=(engine,), min_val=0, max_val=E - 1,
                skip_runtime_bounds_check_because="tile_expert is a minimum with E - 1 of counts")
            return dict(zip(range(a, b), values))

        def logits_bank(t):
            return bank[2 + [a <= t < b for a, b in ROUTED_TOGETHER].index(True)]

        @block.sync
        def _(sp):
            for g, (a, b) in enumerate(GROUPS):
                sp.dma_start(xs[:, a:b, :], x[a:b].rearrange("t p d -> p t d")).then_inc(x_in[g], 16)
                sp.dma_start(mem[:, a:b, :], ctx_mem[a:b].rearrange("t p d -> p t d")).then_inc(mem_in[g], 16)
                if g == 0:
                    sp.dma_start(mask_row[:, :], mask.rearrange("(o t) m -> o (t m)", o=1)).then_inc(mask_in, 16)
            sp.dma_start(wa_sb[:, :, :], wa.rearrange("(c p) e -> p c e", p=P)).then_inc(small_in, 16)
            for row, src in ((0, rgb), (E, sgb), (EA, rb1), (EA + E, sb1)):
                sp.dma_start(bias_rows[row:row + src.shape[0], :], src).then_inc(small_in, 16)
            sp.dma_start(b2_rows[0:E, :], rb2).then_inc(small_in, 16)
            sp.dma_start(b2_rows[E:EA, :], sb2).then_inc(small_in, 16)

            def load_expert(j, g, w1, w2):
                sp.dma_start(wg[:, j, :, :], g.rearrange("o (c p) f -> p (o c) f", p=P)).then_inc(w_in[j], 16)
                sp.dma_start(wu[:, j, :, :], w1.rearrange("o (c p) f -> p (o c) f", p=P)).then_inc(w_in[j], 16)
                sp.dma_start(wd[:, j, :], w2.rearrange("o f d -> f (o d)")).then_inc(w_in[j], 16)

            for j in range(SH):
                load_expert(j, sg[j:j + 1], sw1[j:j + 1], sw2[j:j + 1])
            sp.wait_ge(empty_made, 3)
            sp.dma_start(slots_dram.rearrange("(i p) d -> p i d", p=P),
                         empty[:, :].rearrange("p (o d) -> p o d", o=1).broadcast_to([P, NT, D + 2])
                         ).then_inc(slots_cleared, 16)
            for e in range(0, E, 4):
                for c in range(KC):
                    sp.dma_start(w_gu[:, c, e:e + 4, 0:F],
                                 rg[e:e + 4, c * P:(c + 1) * P, :].rearrange("e p f -> p e f")).then_inc(routed_in, 16)
                    sp.dma_start(w_gu[:, c, e:e + 4, F:2 * F],
                                 rw1[e:e + 4, c * P:(c + 1) * P, :].rearrange("e p f -> p e f")).then_inc(routed_in, 16)
                sp.dma_start(w_d[:, e:e + 4, :], rw2[e:e + 4].rearrange("e f d -> f e d")).then_inc(routed_in, 16)
            for e in range(0, E, E // 2):
                for half, src in enumerate((rgb, rb1)):
                    sp.wait_ge(slots_sent[max(0, e // (E // 2) * 2 + half - 1)], 16 * SENT_TOGETHER)
                    sp.dma_start(bias_gu[:, e:e + E // 2, half * F:(half + 1) * F],
                                 src[e:e + E // 2].rearrange("(o e) f -> o e f", o=1).broadcast_to([P, E // 2, F])
                                 ).then_inc(routed_in, 16)

            def read_slots(n, c):
                t = UNROLL * n + c
                sp.dma_start(slots_in[:, c % SLOT_RING, :],
                             slots_dram[bass.ds(t * P, P), :]).then_inc(slots_read[c % SLOT_RING], 16)

            for i in range(K * T // SENT_TOGETHER):
                sp.wait_ge(slots_sent[i], 16 * SENT_TOGETHER)
            for c in range(SLOT_RING):
                read_slots(0, c)
            turns, rest = divmod(NT - SLOT_RING, UNROLL)
            with sp.Fori(0, turns) as n:
                for c in range(SLOT_RING, SLOT_RING + UNROLL):
                    sp.wait_ge(r_y_made, UNROLL * n + c - SLOT_RING + 1)
                    sp.wait_ge(dest_copied, UNROLL * n + c - SLOT_RING + 1)
                    read_slots(n, c)
            for c in range(NT - rest, NT):
                sp.wait_ge(r_y_made, c - SLOT_RING + 1)
                sp.wait_ge(dest_copied, c - SLOT_RING + 1)
                read_slots(0, c)
            for j in range(RING):
                sp.wait_ge(r_out_sent[j], 16 * len(range(j, NT, RING)))
            for t in range(0, T, 2):
                for k in range(K):
                    sp.dma_start(picked[:, k, t:t + 2, :],
                                 results_dram[(k * T + t) * P:(k * T + t + 2) * P, :].rearrange("(t p) d -> p t d", p=P)
                                 ).then_inc(picked_in[t // 2][k], 16)
            for t in range(0, T, 2):
                sp.wait_ge(picked_added, K * (t + 2))
                sp.dma_start(out[t:t + 2].rearrange("t p d -> p t d"), acc[:, t:t + 2, :]).then_inc(out_done, 16)
            sp.wait_ge(out_done, 16 * T // 2)

        @block.gpsimd
        def _(pool):
            pool.memset(ident[:, :], 0.0).then_inc(ident_made, 1)
            pool.wait_ge(ident_made, 1)
            pool.affine_select(out=ident[:, :], in_=ident[:, :], compare_op=ALU.not_equal, fill=1.0, base=0,
                               pattern=[[-1, P]], channel_multiplier=1).then_inc(ident_made, 1)
            pool.memset(power[:, :], -0.5).then_inc(power_made, 1)
            pool.memset(ones_row[:, :], 1.0).then_inc(ones_made, 1)
            pool.memset(empty[:, 0:D], 0.0).then_inc(empty_made, 1)
            pool.memset(empty[:, :].bitcast(U32)[:, D:D + 1], K * T * P).then_inc(empty_made, 1)
            pool.memset(empty[:, D + 1:D + 2], 0.0).then_inc(empty_made, 1)
            pool.wait_ge(power_made, 1)

            def inverse_deviation(mv, ve, rs, mv_sem, ve_sem, rs_sem, a, b, by):
                pool.wait_ge(mv_sem, b)
                pool.tensor_scalar(ve[:, a:b], mv[:, a:b, 1], EPS, by, ALU.add, ALU.mult).then_inc(ve_sem, 1)
                pool.wait_ge(ve_sem, b // 2)
                pool.tensor_tensor(rs[:, a:b], ve[:, a:b], power[:, a:b], ALU.pow).then_inc(rs_sem, 1)

            for t in range(0, T, 2):
                inverse_deviation(mean_var, var_eps, exp_scale, aggr_made, eps_made, scale1_made, t, t + 2, float(D))
                pool.wait_ge(scale1_made, t // 2 + 1)
                pool.tensor_scalar(neg_scale[:, t:t + 2], exp_scale[:, t:t + 2], -1.0, None,
                                   ALU.mult).then_inc(scale1_negated, 1)
            pool.iota(expert_no[:, :, :], pattern=[[0, T], [1, E]], base=0, channel_multiplier=0,
                      allow_small_or_imprecise_dtypes=True).then_inc(consts, 1)
            pool.memset(combine[:, :, E:EA], 1.0).then_inc(consts, 1)
            pool.memset(ones[:, :], 1.0).then_inc(consts, 1)
            pool.wait_ge(consts, 3)
            pool.affine_select(out=before[:, :], in_=ones[:, :], compare_op=ALU.is_gt, fill=0.0, base=0,
                               pattern=[[1, P]], channel_multiplier=-1).then_inc(consts, 1)
            pool.iota(fill_mark[:, :, :], pattern=[[0, E], [P, T]], base=0, channel_multiplier=0,
                      allow_small_or_imprecise_dtypes=True).then_inc(consts, 1)
            pool.iota(tile_no[:, :, :], pattern=[[1, TILE_NOS], [0, E]], base=0, channel_multiplier=0,
                      allow_small_or_imprecise_dtypes=True).then_inc(consts, 1)
            pool.iota(rows_dest, pattern=[[P, K * T]], base=0, channel_multiplier=1).then_inc(rows_made, 1)
            for t in range(0, T, 2):
                inverse_deviation(mean_var2, var_eps2, rstd2, aggr2_made, eps2_made, rstd2_made, t, t + 2, 1.0)
            for t in range(T):
                pool.wait_ge(hn_made[t % 2], t // 2 + 1)
                pool.tensor_tensor(acc[:, t, :], acc[:, t, :], hn[:, t, :], ALU.add).then_inc(hn_added, 1)
            pool.wait_ge(slots_cleared, 16)
            pool.wait_ge(rows_made, 1 + T)
            pool.wait_ge(share_made, K)
            pool.wait_ge(slot_made, 1)
            for t in range(T):
                for k in range(K):
                    pool.indirect_dma_start(
                        out=slots_dram[:, :], out_offset=bass.IndirectOffsetOnAxis(ap=slot[:, k, t:t + 1], axis=0),
                        in_=rows[:, k, t, :], in_offset=None).then_inc(slots_sent[(K * t + k) // SENT_TOGETHER], 16)

            def copy_dest(n, c):
                t = UNROLL * n + c
                pool.wait_ge(slots_read[c % SLOT_RING], 16 * (n * (UNROLL // SLOT_RING) + c // SLOT_RING + 1))
                if not isinstance(t, int) or t >= RING:
                    pool.wait_ge(r_out_sent[c % RING], 16 * (n * (UNROLL // RING) + c // RING))
                pool.sem_inc(pool_waited, 1)
                pool.tensor_copy(dest[:, c % RING:c % RING + 1],
                                 slots_in[:, c % SLOT_RING, :].bitcast(U32)[:, D:D + 1]).then_inc(dest_copied, 1)

            def send_results(n, c):
                t = UNROLL * n + c
                pool.wait_ge(dest_copied, t + 1)
                pool.wait_ge(r_out_copied, t + 1)
                pool.sem_inc(pool_waited, 1)
                pool.indirect_dma_start(
                    out=results_dram[:, :],
                    out_offset=bass.IndirectOffsetOnAxis(ap=dest[:, c % RING:c % RING + 1], axis=0),
                    in_=r_out[:, c % RING, :], in_offset=None, bounds_check=K * T * P - 1, oob_is_err=False
                ).then_inc(r_out_sent[c % RING], 16)

            def step(n, c):
                s = c if isinstance(n, int) else None
                if s is None or 1 <= s < NT + 1:
                    copy_dest(n, c - 1)
                if s is None or s >= LAST_LAG:
                    send_results(n, c - LAST_LAG)

            for c in range(PEELED):
                step(0, c)
            with pool.Fori(0, TURNS) as n:
                for c in range(PEELED, PEELED + UNROLL):
                    step(n, c)
            for c in range(NT, NT + LAST_LAG):
                step(0, c)

        @block.tensor
        def _(pe):
            def turn_inputs(t):
                for g, (a, _) in enumerate(GROUPS):
                    if t == a:
                        pe.wait_ge(mem_in[g], 16)
                if t >= 4:
                    pe.wait_ge(xm_copied, t - 3)
                for c in range(KC):
                    pe.transpose(bank[XM_BANK[t % 4]][:, (KC + c) * P:(KC + c + 1) * P], mem[:, t, c * P:(c + 1) * P],
                                 ident[:, :])
                pe.wait_ge(xc_made, t + 1)
                for c in range(KC):
                    mm = pe.transpose(bank[XM_BANK[t % 4]][:, c * P:(c + 1) * P], xc[:, t, c * P:(c + 1) * P],
                                      ident[:, :])
                mm.then_inc(xm_turned, 1)

            def score(t):
                pe.wait_ge(xm_copied, t + 1)
                if t >= 4:
                    pe.wait_ge(probs_made, t - 3)
                for c in range(KC):
                    pe.matmul(bank[2 + t % 4][:, 0:P], xm_t[:, t, c, :], xm_t[:, t, KC + c, :],
                              start=(c == 0), stop=False)
                pe.matmul(bank[2 + t % 4][:, 0:P], ones_row[:, :], shut_row[:, t * P:(t + 1) * P],
                          start=False, stop=True).then_inc(scores_made, 1)

            def wait_for_probs(t):
                by_dve = t in PROBS_COPIED_BY[1]
                pe.wait_ge(probs_copied[by_dve], PROBS_COPIED_BY[by_dve].index(t) + 1)

            def turn_probs(t):
                pe.wait_ge(probs_made, t + 1)
                if t >= 3:
                    wait_for_probs(t - 3)
                else:
                    pe.wait_ge(xm_copied, T - 3 + t)
                pe.transpose(bank[PROBS_BANK[t % 3]][:, 0:P], probs[:, t, :], ident[:, :]).then_inc(probs_turned, 1)

            def stay_warm(b, products):
                for i in range(products):
                    pe.matmul(bank[b][:, 0:P], zeros[:, :], zeros[:, :], start=True, stop=True)

            pe.wait_ge(zeros_made, 1)
            stay_warm(6, 8)
            pe.wait_ge(ident_made, 2)
            turn_inputs(0)
            turn_inputs(1)
            pe.wait_ge(ones_made, 1)
            pe.wait_ge(shut_made, 1)
            score(0)
            score(1)
            turn_inputs(2)
            turn_inputs(3)
            for t in range(2, T):
                if t + 2 < T:
                    turn_inputs(t + 2)
                score(t)
                if t >= T - 3:
                    turn_probs(t - (T - 3))

            def read_out(t):
                wait_for_probs(t)
                if t >= 4:
                    pe.wait_ge(h_made, t - 3)
                else:
                    pe.wait_ge(probs_made, t + 5)
                pe.matmul(bank[2 + t % 4][:, 0:D], probs_t[:, t, :], mem[:, t, :],
                          start=True, stop=True).then_inc(read_made, 1)

            for t in range(T):
                if t + 3 < T:
                    turn_probs(t + 3)
                read_out(t)
            pe.wait_ge(small_in, 7 * 16)
            pe.transpose(bank[6][:, 0:2 * EA], bias_rows[:, :], ident[0:2 * EA, 0:2 * EA]).then_inc(bias_turned, 1)

            stay_warm(7, 4)

            def turn_hn(t):
                pe.wait_ge(hn_made[t % 2], t // 2 + 1)
                if t >= 3:
                    pe.wait_ge(hn_copied, t - 2)
                for c in range(KC):
                    mm = pe.transpose(bank[HN_BANK[t % 3]][:, c * P:(c + 1) * P], hn[:, t, c * P:(c + 1) * P],
                                      ident[:, :])
                mm.then_inc(hn_turned, 1)

            def logits(t):
                pe.wait_ge(hn_copied, t + 1)
                for g, (a, _) in enumerate(ROUTED_TOGETHER):
                    if t == a:
                        pe.wait_ge(h_made, T - 3 + g)
                for c in range(KC):
                    mm = pe.matmul(logits_bank(t)[:, t * E:(t + 1) * E], hn_t[:, c, t * P:(t + 1) * P], wa_sb[:, c, :],
                                   start=(c == 0), stop=(c == KC - 1))
                mm.then_inc(logits_made, 1)

            def turn_combine():
                pe.wait_ge(combine_made, 1)
                for t in range(T):
                    mm = pe.transpose(bank[TURNED_BANK[t // 4]][0:EA, (t % 4) * P:(t % 4 + 1) * P], combine[:, t, :],
                                      ident[:, :])
                mm.then_inc(combine_turned, 1)

            def ranks():
                pe.wait_ge(consts, CONSTS)
                pe.wait_ge(taken_made, 1)
                pe.matmul(bank[7][:, 0:T * E], before[:, :], taken[:, :, :], start=True, stop=False,
                          skip_group_check=True)
                for t in range(T):
                    mm = pe.matmul(bank[7][:, (t + 1) * E:(T + 1) * E], ones[:, :],
                                   taken[:, t:t + 1, :].broadcast_to([P, T - t, E]),
                                   start=False, stop=(t == T - 1), skip_group_check=True)
                mm.then_inc(ranks_made, 1)

            def shared_gate(e, h, c):
                mm = pe.matmul(bank[GATE_BANK[e][h]][:, :], wg[:, e, c, :], hn_t[:, c, h * HALF:(h + 1) * HALF],
                               start=(c == 0), stop=(c == KC - 1))
                if c == KC - 1:
                    mm.then_inc(gate_made, 1)

            def shared_up(e, h):
                if e:
                    pe.wait_ge(gelu_made, h + 1)
                for c in range(KC):
                    mm = pe.matmul(bank[UP_BANK[e][h]][:, :], wu[:, e, c, :], hn_t[:, c, h * HALF:(h + 1) * HALF],
                                   start=(c == 0), stop=(c == KC - 1))
                mm.then_inc(up_made, 1)

            def down_place(t):
                return bank[DOWN_BANK[t // 2]][:, (t % 2) * D:(t % 2 + 1) * D]

            def shared_down(e):
                for t in range(T):
                    q, r = t // (T // 2), t % (T // 2)
                    if r == 0:
                        pe.wait_ge(y_made, 2 * e + q + 1)
                        if e == 0:
                            if q == 0:
                                pe.wait_ge(y_made, 2)
                                pe.wait_ge(gelu_made, 2 * SH)
                            else:
                                pe.wait_ge(combine_copied, 2)
                    mm = pe.matmul(down_place(t), y_t[:, q, r * P:(r + 1) * P], wd[:, e, :],
                                   start=(e == 0 and t % 2 == 0), stop=False, skip_group_check=True)
                    if t % 2 and e == 0:
                        mm.then_inc(first_down_made, 1)

            def shared_biases():
                for t in range(T):
                    mm = pe.matmul(down_place(t), combine_t[:, t * P:(t + 1) * P], b2_rows[:, :],
                                   start=False, stop=True, skip_group_check=True)
                    if t % 2:
                        mm.then_inc(shared_made, 1)

            def gate_part(i):
                t, c = divmod(i, KC)
                mm = pe.matmul(bank[GATE_BANK[0][0]][:, t * P:(t + 1) * P], wg[:, 0, c, :],
                               hn_t[:, c, t * P:(t + 1) * P], start=(c == 0), stop=(c == KC - 1))
                if i == KC * T // 2 - 1:
                    mm.then_inc(gate_made, 1)

            turn_hn(0)
            turn_hn(1)
            stay_warm(HN_BANK[2], 3)
            pe.wait_ge(w_in[0], 48)
            for t in range(2, T, 2):
                logits(t - 2)
                turn_hn(t)
                if t == 2:
                    pe.wait_ge(h_made, T)
                if t < T - 2:
                    gate_part(t - 2)
                logits(t - 1)
                turn_hn(t + 1)
                if t < T - 2:
                    gate_part(t - 1)
            logits(T - 2)
            logits(T - 1)

            for i in range(T - 4, KC * T // 2):
                gate_part(i)
            shared_gate(0, 1, 0)
            ranks()
            shared_gate(0, 1, 1)
            pe.wait_ge(bias_copied, 1)
            shared_up(0, 0)
            shared_up(0, 1)
            pe.wait_ge(w_in[1], 48)
            for h in range(2):
                for c in range(KC):
                    shared_gate(1, h, c)
            shared_up(1, 0)
            shared_up(1, 1)
            pe.wait_ge(best_no_made, T)
            pe.wait_ge(route, RANKS_READ)
            turn_combine()
            shared_down(0)
            shared_down(1)
            shared_biases()
            stay_warm(5, 5)

            def turn_slots(n, c):
                t = UNROLL * n + c
                pe.wait_ge(slots_read[c % SLOT_RING], 16 * (n * (UNROLL // SLOT_RING) + c // SLOT_RING + 1))
                if isinstance(t, int) and t < 2:
                    pe.wait_ge(y_made, 2 * SH)
                else:
                    pe.wait_ge(slots_copied, t - 1)
                for k in range(KC):
                    mm = pe.transpose(bank[c % 2][:, k * P:(k + 1) * P], slots_in[:, c % SLOT_RING, k * P:(k + 1) * P],
                                      ident[:, :])
                mm.then_inc(slots_turned, 1)

            def routed_up(n, c, e):
                t = UNROLL * n + c
                pe.wait_ge(slots_copied, t + 1)
                if isinstance(t, int) and t < 2:
                    pe.wait_ge(down_added, T)
                else:
                    pe.wait_ge(r_biased, t - 1)
                for k in range(KC):
                    mm = pe.matmul(bank[2 + c % 2][:, 0:2 * F], slots_t[:, c % 2, k, :],
                                   w_gu[:, k, bass.ds(e, 1), :], start=(k == 0), stop=(k == KC - 1))
                mm.then_inc(r_up_made, 1)

            def routed_down(n, c, e):
                t = UNROLL * n + c
                pe.wait_ge(r_y_copied, t + 1)
                if isinstance(t, int) and t < 2:
                    pe.wait_ge(down_added, T)
                else:
                    pe.wait_ge(r_out_copied, t - 1)
                pe.matmul(bank[6 + c % 2][:, 0:D], r_yt[:, c % 2, :], w_d[:, bass.ds(e, 1), :],
                          start=True, stop=True).then_inc(r_down_made, 1)

            def turn_y(n, c):
                t = UNROLL * n + c
                pe.wait_ge(r_y_made, t + 1)
                if isinstance(t, int) and t < 2:
                    pe.wait_ge(down_added, T)
                else:
                    pe.wait_ge(r_y_copied, t - 1)
                pe.transpose(bank[4 + c % 2][:, 0:P], r_y[:, c % 2, :], ident[:, :]).then_inc(r_y_turned, 1)

            def step(n, c, expert, load=None):
                s = c if isinstance(n, int) else None
                if s is None or s < NT:
                    turn_slots(n, c)
                if load is not None:
                    expert.update(experts_of(PE, n, *load))
                if s is None or 1 <= s < NT + 1:
                    routed_up(n, c - 1, expert[c - 1])
                if s is None or s >= LAST_LAG:
                    routed_down(n, c - LAST_LAG, expert[c - LAST_LAG])
                if s is None or 2 <= s < NT + 2:
                    turn_y(n, c - 2)

            pe.wait_ge(tile_expert_made, 1)
            pe.wait_ge(routed_in, 16 * ROUTED_LOADS)
            expert = experts_of(PE, 0, 0, PEELED - 1)
            for c in range(PEELED):
                step(0, c, expert)
            with pe.Fori(0, TURNS) as n:
                expert = {}
                for c in range(PEELED, PEELED + UNROLL):
                    step(n, c, expert, (PEELED - LAST_LAG, PEELED + UNROLL - 1) if c == PEELED else None)
            expert = experts_of(PE, 0, NT - LAST_LAG, NT)
            for c in range(NT, NT + LAST_LAG):
                step(0, c, expert)

        @block.scalar
        def _(act):
            def copy_inputs(t):
                act.wait_ge(xm_turned, t + 1)
                act.copy(xm_t[:, t, :, :], bank[XM_BANK[t % 4]][:, :]).then_inc(xm_copied, 1)

            def exp_scores(t):
                act.wait_ge(neg_made, t + 1)
                act.activation(probs[:, t, :], bank[2 + t % 4][:, 0:P], ACT.Exp,
                               bias=neg_max[:, t:t + 1], scale=exp_scale[:, t:t + 1],
                               accum_out=prob_sum[:, t:t + 1]).then_inc(probs_made, 1)

            def copy_probs(t):
                act.wait_ge(probs_turned, t + 1)
                act.copy(probs_t[:, t, :], bank[PROBS_BANK[t % 3]][:, 0:P]).then_inc(probs_copied[0], 1)

            for t in range(T + 3):
                if t < T:
                    copy_inputs(t)
                if t >= 3:
                    exp_scores(t - 3)
                if t == T + 1:
                    copy_probs(0)
            for t in PROBS_COPIED_BY[0][1:]:
                copy_probs(t)

            act.wait_ge(bias_turned, 1)
            act.copy(bias_t[:, :], bank[6][:, 0:2 * EA]).then_inc(bias_copied, 1)

            def normalise(t):
                act.wait_ge(shift2_made, t // 2 + 1)
                act.activation(hn[:, t, :], acc[:, t, :], ACT.Identity, bias=shift2[:, t:t + 1],
                               scale=rstd2[:, t:t + 1]).then_inc(hn_made[0], 1)

            def copy_hn(t):
                act.wait_ge(hn_turned, t + 1)
                act.copy(hn_t[:, :, t * P:(t + 1) * P],
                         bank[HN_BANK[t % 3]][:, 0:D].rearrange("p (c s) -> p c s", c=KC)).then_inc(hn_copied, 1)

            def copy_row(t):
                act.copy(rows[:, 1, t, 0:D], hn[:, t, :]).then_inc(rows_made, 1)

            for t in range(T + 1):
                if t % 2 == 0 and t < T:
                    normalise(t)
                if t:
                    copy_hn(t - 1)
                    act.wait_ge(hn_made[(t - 1) % 2], (t - 1) // 2 + 1)
                    copy_row(t - 1)

            act.wait_ge(best_made, T)
            act.activation(exp_neg[:, :, :], best[:, :, 0:K].rearrange("p t k -> p k t"), ACT.Exp,
                           scale=-1.0).then_inc(gate_exp, 1)

            for e in range(SH):
                for h in range(2):
                    act.wait_ge(gate_made, 2 * e + h + 1)
                    if e:
                        act.wait_ge(y_made, h + 1)
                    act.activation(gated[:, h, :], bank[GATE_BANK[e][h]][:, :], ACT.Gelu,
                                   bias=bias_t[:, E + e:E + e + 1]).then_inc(gelu_made, 1)
            act.wait_ge(combine_turned, 1)
            for q in range(2):
                act.copy(combine_t[:, q * HALF:(q + 1) * HALF],
                         bank[TURNED_BANK[q]][0:EA, :]).then_inc(combine_copied, 1)

            def copy_slots(n, c):
                t = UNROLL * n + c
                act.wait_ge(slots_turned, t + 1)
                if not isinstance(t, int) or t >= 2:
                    act.wait_ge(r_up_made, t - 1)
                act.copy(slots_t[:, c % 2, :, :], bank[c % 2][:, 0:D]).then_inc(slots_copied, 1)

            def routed_gelu(n, c):
                t = UNROLL * n + c
                act.wait_ge(r_biased, t + 1)
                if not isinstance(t, int) or t >= 2:
                    act.wait_ge(r_y_made, t - 1)
                act.activation(r_gated[:, c % 2, :], biased[:, c % 2, 0:F], ACT.Gelu).then_inc(r_gelu_made, 1)

            def copy_out(n, c):
                t = UNROLL * n + c
                act.wait_ge(r_down_made, t + 1)
                if not isinstance(t, int) or t >= RING:
                    act.wait_ge(r_out_sent[c % RING], 16 * (n * (UNROLL // RING) + c // RING))
                act.copy(r_out[:, c % RING, :], bank[6 + c % 2][:, 0:D]).then_inc(r_out_copied, 1)

            def step(n, c):
                s = c if isinstance(n, int) else None
                if s is None or s < NT:
                    copy_slots(n, c)
                if s is None or 1 <= s < NT + 1:
                    routed_gelu(n, c - 1)
                if s is None or s >= LAST_LAG:
                    copy_out(n, c - LAST_LAG)

            for c in range(PEELED):
                step(0, c)
            with act.Fori(0, TURNS) as n:
                for c in range(PEELED, PEELED + UNROLL):
                    step(n, c)
            for c in range(NT, NT + LAST_LAG):
                step(0, c)

        @block.vector
        def _(dve):
            def in_turns(steps, a, b):
                for i in range(a, b + len(steps) - 1):
                    for lag, step in enumerate(steps):
                        if a <= i - lag < b:
                            step(i - lag)

            def moments(src, st, st_sem):
                def step(t):
                    dve.bn_stats(st[:, t, :], src[:, t, :]).then_inc(st_sem, 1)
                return step

            def mean_and_var(st, mv, st_sem, mv_sem):
                def step(t):
                    dve.wait_ge(st_sem, t + 1)
                    dve.bn_aggr(mv[:, t, :], st[:, t, :]).then_inc(mv_sem, 1)
                return step

            def center(t):
                dve.wait_ge(aggr_made, t + 1)
                dve.tensor_scalar(xc[:, t, :], xs[:, t, :], mean_var[:, t, 0:1], None,
                                  ALU.subtract).then_inc(xc_made, 1)

            def first_norm(g):
                dve.wait_ge(x_in[g], 16)
                in_turns([moments(xs, stats, stat_made), mean_and_var(stats, mean_var, stat_made, aggr_made),
                          center], *GROUPS[g])

            dve.memset(zeros[:, :], 0.0).then_inc(zeros_made, 1)
            first_norm(0)
            dve.wait_ge(mask_in, 16)
            dve.tensor_scalar(shut_row[:, :], mask_row[:, :], -NEG / SCALE, NEG / SCALE,
                              ALU.mult, ALU.add).then_inc(shut_made, 1)

            def maximum(t):
                dve.wait_ge(scores_made, t + 1)
                dve.tensor_reduce(row_max[:, t:t + 1], bank[2 + t % 4][:, 0:P], AX.X, ALU.max).then_inc(max_made, 1)

            def negated(t):
                dve.wait_ge(max_made, t + 1)
                dve.wait_ge(scale1_negated, t // 2 + 1)
                dve.scalar_tensor_tensor(out=neg_max[:, t:t + 1], in0=row_max[:, t:t + 1], scalar=NEG,
                                         in1=neg_scale[:, t:t + 1], op0=ALU.max, op1=ALU.mult).then_inc(neg_made, 1)

            def copy_probs(t):
                dve.wait_ge(probs_turned, t + 1)
                dve.tensor_copy(probs_t[:, t, :], bank[PROBS_BANK[t % 3]][:, 0:P]).then_inc(probs_copied[1], 1)

            first_norm(1)
            in_turns([maximum, negated], 0, GROUPS[0][1])
            first_norm(2)
            in_turns([maximum, negated], GROUPS[0][1], T - 1)
            copy_probs(1)
            in_turns([maximum, negated], T - 1, T)

            def half(v, g):
                return v[:, g * T // 2:(g + 1) * T // 2]

            def bound_sums(g):
                dve.wait_ge(probs_made, (g + 1) * T // 2)
                dve.tensor_scalar(half(prob_sum, g), half(prob_sum, g), 0.5, None, ALU.max).then_inc(sum_bounded, 1)

            def invert_sums(g):
                dve.wait_ge(sum_bounded, g + 1)
                dve.reciprocal(half(prob_inv, g), half(prob_sum, g)).then_inc(inv_made, 1)

            def readout_factors(g):
                dve.wait_ge(inv_made, g + 1)
                dve.scalar_tensor_tensor(out=half(prob_scale, g), in0=half(row_max, g), scalar=NEG,
                                         in1=half(prob_inv, g), op0=ALU.is_gt, op1=ALU.mult).then_inc(scale_made, 1)

            bound_sums(0)
            invert_sums(0)
            copy_probs(3)
            readout_factors(0)

            def second_half(t):
                if t == 1:
                    bound_sums(1)
                elif t == 2:
                    invert_sums(1)
                elif t == 3:
                    readout_factors(1)

            def add_readout(t):
                dve.wait_ge(read_made, t + 1)
                dve.wait_ge(scale_made, 2 * t // T + 1)
                dve.scalar_tensor_tensor(out=acc[:, t, :], in0=bank[2 + t % 4][:, 0:D],
                                         scalar=prob_scale[:, t:t + 1], in1=xs[:, t, :],
                                         op0=ALU.mult, op1=ALU.add).then_inc(h_made, 1)

            def moments2(t):
                dve.wait_ge(h_made, t + 1)
                moments(acc, stats2, stat2_made)(t)

            def nothing(t):
                pass

            def normalise(t):
                dve.wait_ge(rstd2_made, t // 2 + 1)
                if t % 2 == 0:
                    dve.scalar_tensor_tensor(out=shift2[:, t:t + 1], in0=mean_var2[:, t, 0:1], scalar=-1.0,
                                             in1=rstd2[:, t:t + 1], op0=ALU.mult, op1=ALU.mult).then_inc(shift2_made, 1)
                else:
                    dve.tensor_scalar(hn[:, t, :], acc[:, t, :], mean_var2[:, t, 0:1], rstd2[:, t:t + 1],
                                      ALU.subtract, ALU.mult).then_inc(hn_made[1], 1)

            in_turns([second_half, add_readout, moments2, mean_and_var(stats2, mean_var2, stat2_made, aggr2_made),
                      nothing, normalise], 0, T)

            def largest(t):
                for a, b in ROUTED_TOGETHER:
                    if t == a:
                        dve.wait_ge(logits_made, b)
                dve.max(best[:, t, :], logits_bank(t)[:, t * E:(t + 1) * E]).then_inc(best_made, 1)

            def largest_index(t):
                dve.wait_ge(best_made, t + 1)
                dve.max_index(best_no[:, t, :], best[:, t, :],
                              logits_bank(t)[:, t * E:(t + 1) * E]).then_inc(best_no_made, 1)

            in_turns([largest, largest_index], 0, T)
            step = [0]

            def routed(ins):
                step[0] += 1
                ins.then_inc(route, 1)
                return step[0]

            dve.wait_ge(consts, CONSTS)
            dve.wait_ge(best_no_made, T)
            for k in range(K):
                both_chosen = routed(dve.tensor_tensor(chosen[:, k, :, :], expert_no[:, :, :],
                                                       best_no[:, :, k:k + 1].broadcast_to([P, T, E]), ALU.is_equal))
            dve.wait_ge(route, both_chosen)
            dve.tensor_tensor(taken[:, :, :], chosen[:, 0, :, :], chosen[:, 1, :, :], ALU.add).then_inc(taken_made, 1)
            def over_experts(v):
                return v.rearrange("p (o e) -> p o e", o=1).broadcast_to([P, T, E])

            def over_one(v):
                return v.rearrange("p (t o) -> p t o", o=1)

            dve.wait_ge(gate_exp, 1)
            plus_one = routed(dve.tensor_scalar(one_plus[:, :, :], exp_neg[:, :, :], 1.0, None, ALU.add))
            dve.wait_ge(route, plus_one)
            sigmoid = routed(dve.reciprocal(exp_neg[:, :, :], one_plus[:, :, :]))
            dve.wait_ge(ranks_made, 1)
            counts = bank[7][:, T * E:(T + 1) * E]
            filled = routed(dve.tensor_tensor(fills[:, :, :],
                                              counts.rearrange("p (e o) -> p e o", o=1).broadcast_to([P, E, T]),
                                              fill_mark[:, :, :], ALU.is_gt))
            dve.wait_ge(route, sigmoid)
            summed = routed(dve.tensor_tensor(gate_sum[:, :], exp_neg[:, 0, :], exp_neg[:, 1, :], ALU.add))
            dve.wait_ge(route, filled)
            counted = routed(dve.tensor_reduce(tiles[:, :], fills[:, :, :], AX.X, ALU.add))
            dve.wait_ge(route, summed)
            inverted = routed(dve.reciprocal(gate_inv[:, :], gate_sum[:, :]))
            dve.wait_ge(route, counted)
            ended = routed(dve.tensor_tensor_scan(end[:, :], zeros[:, 0:E], tiles[:, :], 0.0, ALU.add, ALU.add))
            ranked = routed(dve.scalar_tensor_tensor(out=rank_from_end[:, :, :],
                                                     in0=over_experts(tiles[:, :]),
                                                     scalar=-float(P),
                                                     in1=bank[7][:, 0:T * E].rearrange("p (t e) -> p t e", t=T),
                                                     op0=ALU.mult, op1=ALU.add))
            assert ranked == RANKS_READ
            dve.wait_ge(route, inverted)
            for k in range(K):
                dve.tensor_tensor(share[:, k, :, :], over_one(exp_neg[:, k, :]), over_one(gate_inv[:, :]),
                                  ALU.mult).then_inc(share_made, 1)
            dve.wait_ge(route, ranked)
            placed = routed(dve.scalar_tensor_tensor(out=slot_of[:, :, :],
                                                     in0=over_experts(end[:, :]),
                                                     scalar=float(P), in1=rank_from_end[:, :, :],
                                                     op0=ALU.mult, op1=ALU.add))
            dve.wait_ge(route, placed)
            parted = routed(dve.tensor_tensor(slot_part[:, :, :, :].rearrange("p k t e -> p k (t e)"),
                                              chosen[:, :, :, :].rearrange("p k t e -> p k (t e)"),
                                              slot_of[:, :, :].rearrange("p (o t) e -> p o (t e)", o=1)
                                              .broadcast_to([P, K, T * E]),
                                              ALU.mult))
            dve.wait_ge(route, parted)
            with nc.allow_low_precision(reason="whole numbers below 2 ** 24"):
                dve.tensor_reduce(slot[:, :, :], slot_part[:, :, :, :], AX.X, ALU.add).then_inc(slot_made, 1)
            passed = routed(dve.tensor_tensor(past[:, :, :],
                                              end[0:1, :].rearrange("p (o e) -> p o e", o=1)
                                              .broadcast_to([1, TILE_NOS, E]),
                                              tile_no[:, :, :], ALU.is_le))
            dve.wait_ge(share_made, K)
            for k in range(K):
                parts_made = routed(dve.tensor_tensor(part[:, k, :, :], chosen[:, k, :, :],
                                                      share[:, k, :, :].broadcast_to([P, T, E]), ALU.mult))
            dve.wait_ge(route, passed)
            found = routed(dve.tensor_reduce(tile_expert_f[:, :], past[:, :, :], AX.X, ALU.add))
            dve.wait_ge(route, parts_made)
            dve.tensor_tensor(combine[:, :, 0:E], part[:, 0, :, :], part[:, 1, :, :],
                              ALU.add).then_inc(combine_made, 1)
            dve.wait_ge(route, found)
            dve.tensor_scalar(tile_expert[:, :], tile_expert_f[:, :], float(E - 1), None,
                              ALU.min).then_inc(tile_expert_made, 1)

            for e in range(SH):
                for h in range(2):
                    dve.wait_ge(up_made, 2 * e + h + 1)
                    dve.wait_ge(gelu_made, 2 * e + h + 1)
                    if e:
                        dve.wait_ge(first_down_made, 2 * (h + 1))
                    dve.scalar_tensor_tensor(out=y_t[:, h, :], in0=bank[UP_BANK[e][h]][:, :],
                                             scalar=bias_t[:, EA + E + e:EA + E + e + 1], in1=gated[:, h, :],
                                             op0=ALU.add, op1=ALU.mult).then_inc(y_made, 1)
            for t in range(T):
                dve.wait_ge(shared_made, t // 2 + 1)
                dve.wait_ge(hn_added, t + 1)
                dve.tensor_tensor(acc[:, t, :], bank[DOWN_BANK[t // 2]][:, (t % 2) * D:(t % 2 + 1) * D], acc[:, t, :],
                                  ALU.add).then_inc(down_added, 1)

            def add_bias(n, c, e):
                t = UNROLL * n + c
                dve.wait_ge(r_up_made, t + 1)
                if not isinstance(t, int) or t >= 2:
                    dve.wait_ge(r_y_made, t - 1)
                dve.tensor_tensor(biased[:, c % 2, :], bank[2 + c % 2][:, 0:2 * F],
                                  bias_gu[:, bass.ds(e, 1), :].rearrange("p o f -> p (o f)"),
                                  ALU.add).then_inc(r_biased, 1)

            def multiply(n, c):
                t = UNROLL * n + c
                dve.wait_ge(r_biased, t + 1)
                dve.wait_ge(r_gelu_made, t + 1)
                if not isinstance(t, int) or t >= 2:
                    dve.wait_ge(r_y_turned, t - 1)
                dve.scalar_tensor_tensor(out=r_y[:, c % 2, :], in0=r_gated[:, c % 2, :],
                                         scalar=slots_in[:, c % SLOT_RING, D + 1:D + 2], in1=biased[:, c % 2, F:2 * F],
                                         op0=ALU.mult, op1=ALU.mult).then_inc(r_y_made, 1)

            def copy_y(n, c):
                t = UNROLL * n + c
                dve.wait_ge(r_y_turned, t + 1)
                if not isinstance(t, int) or t >= 2:
                    dve.wait_ge(r_down_made, t - 1)
                dve.tensor_copy(r_yt[:, c % 2, :], bank[4 + c % 2][:, 0:P]).then_inc(r_y_copied, 1)

            def step(n, c, expert):
                s = c if isinstance(n, int) else None
                if s is None or 1 <= s < NT + 1:
                    add_bias(n, c - 1, expert[c - 1])
                if s is None or 2 <= s < NT + 2:
                    copy_y(n, c - 2)
                if s is None or 1 <= s < NT + 1:
                    multiply(n, c - 1)

            dve.wait_ge(tile_expert_made, 1)
            dve.wait_ge(routed_in, 16 * ROUTED_LOADS)
            expert = experts_of(DVE, 0, 0, PEELED - 1)
            for c in range(PEELED):
                step(0, c, expert)
            with dve.Fori(0, TURNS) as n:
                expert = experts_of(DVE, n, PEELED - 1, PEELED + UNROLL - 1)
                for c in range(PEELED, PEELED + UNROLL):
                    step(n, c, expert)
            expert = experts_of(DVE, 0, NT - 1, NT)
            for c in range(NT, NT + LAST_LAG):
                step(0, c, expert)

            for a in range(0, T, 2):
                for k in range(K):
                    dve.wait_ge(picked_in[a // 2][k], 16)
                    for t in range(a, a + 2):
                        if k == 0:
                            dve.wait_ge(down_added, t + 1)
                        else:
                            dve.wait_ge(picked_added, K * a + t - a + 1)
                        dve.tensor_tensor(acc[:, t, :], picked[:, k, t, :], acc[:, t, :],
                                          ALU.add).then_inc(picked_added, 1)


_INS = ["x", "ctx_2048", "mask_BxS2_bk0", "L0_ffn_wa", "L0_ffn_rg", "L0_ffn_rgb", "L0_ffn_rw1", "L0_ffn_rb1",
        "L0_ffn_rw2", "L0_ffn_rb2", "L0_ffn_sg", "L0_ffn_sgb", "L0_ffn_sw1", "L0_ffn_sb1", "L0_ffn_sw2",
        "L0_ffn_sb2"]
_OUTS = [((8, 128, 256), "float32")]


def kernel(**inputs):
    import numpy as _np
    import concourse.bacc as _bacc
    from concourse import mybir as _mybir
    from concourse.bass_utils import run_bass_kernel_spmd as _run

    nc = _bacc.Bacc("TRN2", target_bir_lowering=False, num_devices=1)
    arrays, args = {}, []
    for name in _INS:
        a = _np.ascontiguousarray(inputs[name])
        arrays[f"in_{name}_dram"] = a
        args.append(nc.dram_tensor(f"in_{name}_dram", a.shape, _mybir.dt.from_np(a.dtype), kind="ExternalInput").ap())
    for i, (shape, dtype) in enumerate(_OUTS):
        dt = _mybir.dt.from_np(_np.dtype(dtype))
        args.append(nc.dram_tensor(f"out_{i}_dram", shape, dt, kind="ExternalOutput").ap())
    xattn_moe(nc, *args)
    r = _run(nc, [arrays], core_ids=[0])
    got = tuple(r.results[0][f"out_{i}_dram"] for i in range(len(_OUTS)))
    return got[0]
```
